# Optimizing a Trainium2 kernel written in Bass

```python
import numpy as np
import jax
import jax.numpy as jnp

def _softmax(x, axis=-1):
    return jax.nn.softmax(x, axis=axis)

def _gelu(x):
    return jax.nn.gelu(x, approximate=True)

def _silu(x):
    return jax.nn.silu(x)

def _sigmoid(x):
    return jax.nn.sigmoid(x)

def _layernorm(x, axis=-1, eps=1e-05):
    m = jnp.mean(x, axis=axis, keepdims=True)
    v = jnp.var(x, axis=axis, keepdims=True)
    return (x - m) / jnp.sqrt(v + eps)

def _scatter_add(tgt, idx, src, axis=0):
    return tgt.at[idx].add(src)

def _segment_sum(src, seg, n):
    return jax.ops.segment_sum(src, seg, n)
kernel_name = 'mk_adaln_d1_jaxref_r4_2e6611'

def setup_inputs(seed: int=0):
    np.random.seed(seed)
    _w = jnp.asarray

    def _L0_attn_setup():
        import jax, jax.numpy as jnp
        import numpy as np
        DIM = 256
        NUM_HEADS = 16
        HD = DIM // NUM_HEADS
        ROPE_DIM = 64
        ROPE_BASE = 10000.0

        def _apply_rope(t):
            D = t.shape[-1]
            N = t.shape[2]
            pos = jnp.arange(N, dtype=t.dtype)
            inv = 1.0 / ROPE_BASE ** (jnp.arange(0, D, 2, dtype=t.dtype) / D)
            freqs = pos[:, None] * inv[None, :]
            cos = jnp.cos(freqs)[None, None]
            sin = jnp.sin(freqs)[None, None]
            e = t[..., 0::2]
            o = t[..., 1::2]
            eo = e * cos - o * sin
            oo = e * sin + o * cos
            return jnp.stack([eo, oo], axis=-1).reshape(t.shape)
        key = jax.random.key(seed)
        ks = jax.random.split(key, 5)
        B, N = (2, 512)
        s = 0.02
        return {'x': jax.random.normal(ks[0], (B, N, DIM), dtype=jnp.float32), 'qkv_w': jax.random.normal(ks[1], (3 * DIM, DIM), dtype=jnp.float32) * s, 'qkv_b': jax.random.normal(ks[2], (3 * DIM,), dtype=jnp.float32) * s, 'proj_w': jax.random.normal(ks[3], (DIM, DIM), dtype=jnp.float32) * s, 'proj_b': jax.random.normal(ks[4], (DIM,), dtype=jnp.float32) * s}
    _L0_attn_in = _L0_attn_setup()

    def _L0_ffn_setup():
        import jax, jax.numpy as jnp
        import numpy as np
        H = 256
        M = 128
        E = 16
        TOP_K = 4
        N_GROUP = 4
        TOPK_GROUP = 2
        SCALE = 2.5
        B, S = (2, 256)

        def _gate(x2d, gate_kernel, gate_bias):
            n = x2d.shape[0]
            logits = jnp.dot(x2d.astype(jnp.float32), gate_kernel.astype(jnp.float32))
            scores = jax.nn.sigmoid(logits)
            scores_for_choice = scores + gate_bias
            group_scores = scores_for_choice.reshape(n, N_GROUP, E // N_GROUP)
            top2 = jax.lax.top_k(group_scores, k=2)[0]
            group_sum = jnp.sum(top2, axis=-1)
            group_idx = jax.lax.top_k(group_sum, k=TOPK_GROUP)[1]
            group_mask = jnp.zeros_like(group_sum).at[jnp.arange(n)[:, None], group_idx].set(1.0)
            score_mask = jnp.repeat(group_mask[:, :, None], E // N_GROUP, axis=2).reshape(n, E)
            masked_scores = jnp.where(score_mask > 0, scores_for_choice, 0.0)
            topk_weight, topk_idx = jax.lax.top_k(masked_scores, k=TOP_K)
            topk_weight = topk_weight / (jnp.sum(topk_weight, axis=-1, keepdims=True) + 1e-20)
            topk_weight = topk_weight * SCALE
            return (topk_idx, topk_weight)
        key = jax.random.key(seed)
        ks = jax.random.split(key, 9)
        sc_h = 1.0 / np.sqrt(H)
        sc_m = 1.0 / np.sqrt(M)
        return {'hidden_states': jax.random.normal(ks[0], (B, S, H), jnp.float32), 'gate_kernel': jax.random.normal(ks[1], (H, E), jnp.float32) * sc_h, 'gate_bias': jax.random.normal(ks[2], (E,), jnp.float32) * 0.01, 'w_gate': jax.random.normal(ks[3], (E, H, M), jnp.float32) * sc_h, 'w_up': jax.random.normal(ks[4], (E, H, M), jnp.float32) * sc_h, 'w_down': jax.random.normal(ks[5], (E, M, H), jnp.float32) * sc_m, 'sw_gate': jax.random.normal(ks[6], (H, 2 * M), jnp.float32) * sc_h, 'sw_up': jax.random.normal(ks[7], (H, 2 * M), jnp.float32) * sc_h, 'sw_down': jax.random.normal(ks[8], (2 * M, H), jnp.float32) * (1.0 / np.sqrt(2 * M))}
    _L0_ffn_in = _L0_ffn_setup()
    _L0_c = _w((lambda *s: np.random.randn(*s).astype(np.float32) * 0.05)(16, 256))
    _L0_wmod = _w((lambda *s: np.random.randn(*s).astype(np.float32) * 0.05)(256, 6 * 256) * 256 ** (-0.5))
    _d = {'L0_attn_x': _L0_attn_in['x'], 'L0_attn_qkv_w': _L0_attn_in['qkv_w'], 'L0_attn_qkv_b': _L0_attn_in['qkv_b'], 'L0_attn_proj_w': _L0_attn_in['proj_w'], 'L0_attn_proj_b': _L0_attn_in['proj_b'], 'L0_ffn_gate_kernel': _L0_ffn_in['gate_kernel'], 'L0_ffn_gate_bias': _L0_ffn_in['gate_bias'], 'L0_ffn_w_gate': _L0_ffn_in['w_gate'], 'L0_ffn_w_up': _L0_ffn_in['w_up'], 'L0_ffn_w_down': _L0_ffn_in['w_down'], 'L0_ffn_sw_gate': _L0_ffn_in['sw_gate'], 'L0_ffn_sw_up': _L0_ffn_in['sw_up'], 'L0_ffn_sw_down': _L0_ffn_in['sw_down'], 'L0_c': _L0_c, 'L0_wmod': _L0_wmod}
    _x0 = _d['L0_attn_x']
    _d['L0_attn_x'] = jax.random.normal(jax.random.fold_in(jax.random.key(seed), 1), (16, 512, 256), dtype=_x0.dtype)
    del _x0
    return _d

def reference(L0_attn_x, L0_attn_qkv_w, L0_attn_qkv_b, L0_attn_proj_w, L0_attn_proj_b, L0_ffn_gate_kernel, L0_ffn_gate_bias, L0_ffn_w_gate, L0_ffn_w_up, L0_ffn_w_down, L0_ffn_sw_gate, L0_ffn_sw_up, L0_ffn_sw_down, L0_c, L0_wmod):

    def _L0_attn_ref(x, qkv_w, qkv_b, proj_w, proj_b):
        import jax, jax.numpy as jnp
        import numpy as np
        DIM = 256
        NUM_HEADS = 16
        HD = DIM // NUM_HEADS
        ROPE_DIM = 64
        ROPE_BASE = 10000.0

        def _apply_rope(t):
            D = t.shape[-1]
            N = t.shape[2]
            pos = jnp.arange(N, dtype=t.dtype)
            inv = 1.0 / ROPE_BASE ** (jnp.arange(0, D, 2, dtype=t.dtype) / D)
            freqs = pos[:, None] * inv[None, :]
            cos = jnp.cos(freqs)[None, None]
            sin = jnp.sin(freqs)[None, None]
            e = t[..., 0::2]
            o = t[..., 1::2]
            eo = e * cos - o * sin
            oo = e * sin + o * cos
            return jnp.stack([eo, oo], axis=-1).reshape(t.shape)
        B, N, C = x.shape
        H, D = (NUM_HEADS, HD)
        scale = D ** (-0.5)
        qkv = x @ qkv_w.T + qkv_b
        qkv = qkv.reshape(B, N, 3, H, D).transpose(2, 0, 3, 1, 4)
        q, k, v = (qkv[0], qkv[1], qkv[2])
        q = jnp.concatenate([_apply_rope(q[..., :ROPE_DIM]), q[..., ROPE_DIM:]], axis=-1)
        k = jnp.concatenate([_apply_rope(k[..., :ROPE_DIM]), k[..., ROPE_DIM:]], axis=-1)
        attn = jnp.einsum('bhnd,bhmd->bhnm', q, k) * scale
        attn = jax.nn.softmax(attn, axis=-1)
        out = jnp.einsum('bhnm,bhmd->bhnd', attn, v)
        out = out.transpose(0, 2, 1, 3).reshape(B, N, C)
        return out @ proj_w.T + proj_b

    def _L0_ffn_ref(hidden_states, gate_kernel, gate_bias, w_gate, w_up, w_down, sw_gate, sw_up, sw_down):
        import jax, jax.numpy as jnp
        import numpy as np
        H = 256
        M = 128
        E = 16
        TOP_K = 4
        N_GROUP = 4
        TOPK_GROUP = 2
        SCALE = 2.5
        B, S = (2, 256)

        def _gate(x2d, gate_kernel, gate_bias):
            n = x2d.shape[0]
            logits = jnp.dot(x2d.astype(jnp.float32), gate_kernel.astype(jnp.float32))
            scores = jax.nn.sigmoid(logits)
            scores_for_choice = scores + gate_bias
            group_scores = scores_for_choice.reshape(n, N_GROUP, E // N_GROUP)
            top2 = jax.lax.top_k(group_scores, k=2)[0]
            group_sum = jnp.sum(top2, axis=-1)
            group_idx = jax.lax.top_k(group_sum, k=TOPK_GROUP)[1]
            group_mask = jnp.zeros_like(group_sum).at[jnp.arange(n)[:, None], group_idx].set(1.0)
            score_mask = jnp.repeat(group_mask[:, :, None], E // N_GROUP, axis=2).reshape(n, E)
            masked_scores = jnp.where(score_mask > 0, scores_for_choice, 0.0)
            topk_weight, topk_idx = jax.lax.top_k(masked_scores, k=TOP_K)
            topk_weight = topk_weight / (jnp.sum(topk_weight, axis=-1, keepdims=True) + 1e-20)
            topk_weight = topk_weight * SCALE
            return (topk_idx, topk_weight)
        orig_shape = hidden_states.shape
        x = hidden_states.reshape(-1, orig_shape[-1])
        topk_idx, topk_weight = _gate(x, gate_kernel, gate_bias)
        onehot = (topk_idx[:, :, None] == jnp.arange(E)[None, None, :]).astype(topk_weight.dtype)
        combine = jnp.einsum('nke,nk->ne', onehot, topk_weight)
        g = jnp.einsum('nh,ehm->enm', x, w_gate)
        u = jnp.einsum('nh,ehm->enm', x, w_up)
        inter = jax.nn.silu(g) * u
        y_e = jnp.einsum('enm,emh->enh', inter, w_down)
        y = jnp.einsum('ne,enh->nh', combine, y_e)
        shared = jnp.dot(jax.nn.silu(jnp.dot(x, sw_gate)) * jnp.dot(x, sw_up), sw_down)
        return (y + shared).reshape(orig_shape)
    x = L0_attn_x
    mod = (_silu(L0_c) @ L0_wmod).reshape(L0_c.shape[0], 6, 1, -1)
    sa, ca, ga, sb, cb, gb = (mod[:, 0], mod[:, 1], mod[:, 2], mod[:, 3], mod[:, 4], mod[:, 5])
    ga = (2 * (ga >= 0) - 1) * jnp.maximum(jnp.abs(ga), 0.25)
    gb = (2 * (gb >= 0) - 1) * jnp.maximum(jnp.abs(gb), 0.25)
    h = _layernorm(x, axis=-1) * (1 + ca) + sa
    x = x + ga * _L0_attn_ref(h, L0_attn_qkv_w, L0_attn_qkv_b, L0_attn_proj_w, L0_attn_proj_b)
    h = _layernorm(x, axis=-1) * (1 + cb) + sb
    x = x + gb * _L0_ffn_ref(h, L0_ffn_gate_kernel, L0_ffn_gate_bias, L0_ffn_w_gate, L0_ffn_w_up, L0_ffn_w_down, L0_ffn_sw_gate, L0_ffn_sw_up, L0_ffn_sw_down)
    return x

_drawn_inputs = setup_inputs


def setup_inputs(seed=0):
    import zlib

    import numpy as np

    out = dict(_drawn_inputs(seed))
    spreads = {}
    factors = {'L0_attn_qkv_w': 8.0,
     'L0_attn_qkv_b': 7.368,
     'L0_attn_proj_w': 6.954,
     'L0_attn_proj_b': 12.203}
    for name, (base, spread) in spreads.items():
        noise = np.random.default_rng([zlib.crc32(name.encode()), seed]).standard_normal(out[name].shape)
        drawn = base * np.exp(spread * noise) if base else spread * noise
        out[name] = jnp.asarray(drawn.astype(out[name].dtype))
    for name, factor in factors.items():
        out[name] = (out[name] * factor).astype(out[name].dtype)
    return out
```

```python
from contextlib import ExitStack

import numpy as np

import concourse.bass as bass
from concourse import mybir

F32 = mybir.dt.float32
F32R = mybir.dt.float32r
BF16 = mybir.dt.bfloat16
ALU = mybir.AluOpType
ACT = mybir.ActivationFunctionType
AX = mybir.AxisListType

P = 128
NB, N, C = 16, 512, 256
H, HD = 16, 16
HALF = HD // 2
E, M = 16, 128
SLOTS = E + 2
TT = N // P
CT = C // P
Q4 = H // 4
LN_EPS = 1e-5
TOPK_EPS = 1e-20
ROUTE_SCALE = 2.5
GATE_MIN = 0.25
SM_SCALE = float(HD) ** -0.5
CONST_DMAS = 11
SENTINEL = -3.0e38

Q_PART = (0, 0, 1, 1, 0, 2)
K_PART = (0, 1, 0, 1, 2, 0)
GROUPS = len(Q_PART)
ROWS = GROUPS * HD
SHIFT_ROWS = 2

SA, CA, GA, GPB, SB, CB, GB = range(0, 14, 2)
MODS = 14

PAIRS = H * TT // 2
RING = PAIRS + 2
TILES = H * TT
GRP = TILES // 4
LN_STEPS = 3 * TT + 1
ROPE_STEPS = 28
NORM_STEPS = 3
RT_STEPS = 32
STACK_DMAS = 2 * 2 * GROUPS
MAX_SLOTS = range(1, 9)
EXP_SLOTS = range(9, 17)


def build(nc, x, cT, wmod, wqkv, qkb, vb, pw, pb, gk, gb, wffn, cosT, sinT, ident_in, tri_in, out):
    ctx = ExitStack()
    with ctx:
        def sb(name, shape, dt=F32):
            return ctx.enter_context(nc.sbuf_tensor(name, shape, dt))

        def sem(name):
            return ctx.enter_context(nc.semaphore(name))

        wgu_hi = sb("wgu_hi", [P, SLOTS, 2, CT, M], F32R)
        wgu_lo = sb("wgu_lo", [P, SLOTS, 2, CT, M], BF16)
        wd_hi = sb("wd_hi", [P, SLOTS, C], F32R)
        wd_lo = sb("wd_lo", [P, SLOTS, C], BF16)
        wqkv_hi = sb("wqkv_hi", [P, CT, 3 * C], F32R)
        wqkv_lo = sb("wqkv_lo", [P, CT, 3 * C], BF16)
        pw_s = sb("pw_s", [P, Q4, C])
        cos_s = sb("cos_s", [P, N])
        sin_s = sb("sin_s", [P, N])
        ident = sb("ident", [P, P])
        ident_b = sb("ident_b", [P, P], BF16)
        gk_s = sb("gk_s", [P, CT, E])
        gb_s = sb("gb_s", [P, E])
        vb_s = sb("vb_s", [P, C])
        qkb_s = sb("qkb_s", [P, 4])
        pb_s = sb("pb_s", [P, CT])
        tri = sb("tri", [P, 16])
        mhalf = sb("mhalf", [P, TT])
        modB = sb("modB", [P, NB * MODS])

        qs = sb("qs", [P, H, N], BF16)
        ks = sb("ks", [P, H, N], BF16)
        pt = sb("pt", [P, 2, 4, N])
        v_s = sb("v_s", [P, TT, H, 32])
        on = sb("on", [P, Q4, N])
        nrm = sb("nrm", [P, 2, N])
        xa = sb("xa", [P, TT, C])
        x2 = sb("x2", [P, TT, C])
        hf = sb("hf", [P, CT, N])
        h_hi = sb("h_hi", [P, CT, N], F32R)
        h_lo = sb("h_lo", [P, CT, N], F32R)
        cb = sb("cb", [P, 3, N])
        th = sb("th", [P, N])
        ff = sb("ff", [P, 2, N])
        in_hi = sb("in_hi", [P, N], F32R)
        in_lo = sb("in_lo", [P, N], F32R)
        mx = sb("mx", [P, TILES])
        m12 = sb("m12", [P, 2, 2, 32], BF16)
        mT = sb("mT", [32, 2, 2, P], BF16)
        st1, st2 = sb("st1", [P, TT, 6]), sb("st2", [P, TT, 6])
        mv1, mv2 = sb("mv1", [P, TT, 2]), sb("mv2", [P, TT, 2])
        ve1, ve2 = sb("ve1", [P, TT]), sb("ve2", [P, TT])
        rstd1, rstd2 = sb("rstd1", [P, TT]), sb("rstd2", [P, TT])
        rv = sb("rv", [P, TT, E])
        comb = sb("comb", [P, TT, E])

        cd = nc.dram_tensor("combine_rows", [E, N], F32, kind="Internal").ap()

        S = [ctx.enter_context(nc.psum_tensor(f"S{i}", [P, N], F32)) for i in range(4)]
        G = ctx.enter_context(nc.psum_tensor("G", [P, N], F32))
        U = ctx.enter_context(nc.psum_tensor("U", [P, N], F32))
        Y = [ctx.enter_context(nc.psum_tensor(f"Y{i}", [P, N], F32)) for i in range(2)]
        O = S[3]

        wmod_v = qs[:, :, :].rearrange("p h n -> p (h n)").bitcast(F32)[:, 0:CT * 6 * C] \
            .rearrange("p (c n) -> p c n", c=CT)
        ptf = pt[:, :, :, :].rearrange("p a b n -> p (a b) n")
        wqkv_v = pt[:, :, :, :].rearrange("p a b n -> p (a b n)")[:, 0:CT * 3 * C] \
            .rearrange("p (c n) -> p c n", c=CT)
        parts = [ptf[:, 3 * t:3 * t + 3, :].rearrange("p a n -> p (a n)").bitcast(BF16)
                 .rearrange("p (j r n) -> p j r n", j=3, r=2) for t in range(2)]
        rope_a, rope_b = ptf[:, 6, :], ptf[:, 7, :]
        scratch = on[:, :, :].rearrange("p q n -> p (q n)")
        at = [0]

        def cut(*shape):
            n = int(np.prod(shape))
            v = scratch[:, at[0]:at[0] + n]
            at[0] += n
            names = "abc"[:len(shape)]
            return v.rearrange(f"p ({' '.join(names)}) -> p {' '.join(names)}",
                               **dict(zip(names[1:], shape[1:]))) if len(shape) > 1 else v

        rp, rq = cut(4 * TT, 2), cut(4 * TT, 2)
        rs_ = cut(5, 4 * TT)
        rk = cut(2, 16 * TT)
        rw, rr = cut(TT, E + 4), cut(TT, E + 4)
        r8 = cut(TT, 8)
        rsel = cut(TT, E)
        rsum = cut(3, TT)
        stage = [x2[:, :, :].rearrange("p t c -> p (t c)"), ff[:, :, :].rearrange("p a n -> p (a n)")]

        def upper(ap):
            return ap.bitcast(BF16)[:, 1::2]

        s_const = sem("s_const")
        s_wmod, s_wq, s_x0 = sem("s_wmod"), sem("s_wq"), sem("s_x0")
        s_pre = sem("s_pre")
        s_cact = sem("s_cact")
        s_modp = sem("s_modp")
        s_stage = [sem("s_stage0"), sem("s_stage1")]
        s_whi = sem("s_whi")
        s_wlo = sem("s_wlo")
        s_xln = sem("s_xln")
        s_xres = sem("s_xres")
        s_ln1, s_ln2 = sem("s_ln1"), sem("s_ln2")
        s_rstd = sem("s_rstd")
        s_rstd2 = sem("s_rstd2")
        s_ht1, s_ht2 = sem("s_ht1"), sem("s_ht2")
        s_he1, s_he2 = sem("s_he1"), sem("s_he2")
        s_hs1, s_hs2 = sem("s_hs1"), sem("s_hs2")
        s_qk = sem("s_qk")
        s_v = sem("s_v")
        s_vb = sem("s_vb")
        s_rope = sem("s_rope")
        s_stk = sem("s_stk")
        s_smx = sem("s_smx")
        s_rd = sem("s_rd")
        s_mm = sem("s_mm")
        s_mrow = sem("s_mrow")
        s_st = sem("s_st")
        s_ex = sem("s_ex")
        s_pv = sem("s_pv")
        s_oc = sem("s_oc")
        s_nm = sem("s_nm")
        s_pj = sem("s_pj")
        s_ae = sem("s_ae")
        s_at = sem("s_at")
        s_rs = sem("s_rs")
        s_lg = sem("s_lg")
        s_la = sem("s_la")
        s_rt = sem("s_rt")
        s_ct = sem("s_ct")
        s_ce = sem("s_ce")
        s_cdw = sem("s_cdw")
        s_cb = [sem(f"s_cb{i}") for i in range(3)]
        cb_uses = [len(range(i, E, 3)) for i in range(3)]
        s_g, s_u = sem("s_g"), sem("s_u")
        s_fa = sem("s_fa")
        s_fd = sem("s_fd")
        s_fp = sem("s_fp")
        s_dn = sem("s_dn")
        s_ye = sem("s_ye")
        s_yt = sem("s_yt")
        s_ya = sem("s_ya")
        s_out = sem("s_out")

        def later(b):
            return not isinstance(b, int) or b > 0

        x_t = x.rearrange("b (t p) c -> b p t c", p=P)
        out_t = out.rearrange("b (t p) c -> b p t c", p=P)

        ring = [("pair", p) for p in range(18)] + [("rows", 0)] + [("pair", p) for p in range(18, PAIRS)]
        per_slot = -(-len(ring) // len(MAX_SLOTS))
        ring_of = {e: ring[i * per_slot:(i + 1) * per_slot] for i, e in enumerate(MAX_SLOTS)}
        ring_at = {item: i for i, item in enumerate(ring)}
        ring_at[("rows", 1)] = len(ring)
        grp_per_slot = GRP // len(EXP_SLOTS)
        groups_of = {e: range(i * grp_per_slot, (i + 1) * grp_per_slot) for i, e in enumerate(EXP_SLOTS)}

        block = ctx.enter_context(nc.Block())

        @block.sync
        def _(sp):
            def load_cb(f, e):
                if e < 3:
                    sp.wait_ge(s_cdw, 16 * f + 16)
                    sp.nop(nofuse=True)
                    last = max(k for k in range(E) if k % 3 == e)
                    if later(f):
                        sp.wait_ge(s_fp, 2 * SLOTS * (f - 1) + 2 * last + 1)
                else:
                    sp.wait_ge(s_fp, 2 * SLOTS * f + 2 * (e - 3) + 1)
                sp.dma_start(cb[:, e % 3, :], cd[e, :].partition_broadcast(P)).then_inc(s_cb[e % 3], 16)

            def load_x_ln(n):
                sp.dma_start(xa[:, :, :], x_t[n]).then_inc(s_xln, 16)

            def shift_rows(b, half):
                sp.wait_ge(s_rd, RING * b + ring_at[("rows", half)] + 1)
                for part in range(SHIFT_ROWS):
                    dst = qs[ROWS + part:ROWS + part + 1, half * 8:half * 8 + 8, :] \
                        .rearrange("o h n -> o (h n)").rearrange("o (r q) -> o r q", q=P)
                    sp.dma_start(dst, mT[:, half, part, :]).then_inc(s_mrow, 16)

            def stack(n, t):
                for r in range(2):
                    sp.wait_ge(s_rope, ROPE_STEPS * n + 14 * t + 7 * (r + 1))
                    for g in range(GROUPS):
                        row = g * HD + r * HALF
                        dst = (qs, ks)[t][row:row + HALF, :, :]
                        src = parts[t][:, (Q_PART, K_PART)[t][g], r, :]
                        sp.dma_start(dst, src).then_inc(s_stk, 16)

            def iteration(b, first=False, last=False):
                f = b - 1
                for e in range(SLOTS):
                    if first:
                        if e >= 2:
                            sp.wait_ge(s_wlo, 2 * (e - 1))
                        sp.dma_start(stage[e % 2][:, 0:768], wffn[e]).then_inc(s_stage[e % 2], 16)
                    elif e + 2 < E and e > 0:
                        load_cb(f, e + 2)
                    if e == 5:
                        if not last:
                            if first:
                                sp.wait_ge(s_ht1, 2)
                            else:
                                sp.wait_ge(s_ht2, 2 * f + 2)
                                sp.nop(nofuse=True)
                            load_x_ln(b + 1)
                    if e == 6:
                        shift_rows(b, 0)
                    if e == 9:
                        shift_rows(b, 1)
                tail(b, first, last)

            def tail(b, first, last):
                if last:
                    sp.wait_ge(s_ht2, 2 * b)
                    sp.nop(nofuse=True)
                else:
                    sp.wait_ge(s_ht1, 2 * b + 4)
                    sp.nop(nofuse=True)
                sp.dma_start(xa[:, :, :], x_t[b]).then_inc(s_xres, 16)
                if not first:
                    store(b - 1)
                if not last:
                    stack(b + 1, 0)
                if not last:
                    stack(b + 1, 1)
                combine_rows(b)

            def combine_rows(b):
                sp.wait_ge(s_ce, b + 1)
                sp.nop(nofuse=True)
                for i in range(3):
                    if later(b):
                        sp.wait_ge(s_cb[i], 16 * cb_uses[i] * b)
                        sp.nop(nofuse=True)
                sp.dma_start(cd, nrm[0:E, 1, :]).then_inc(s_cdw, 16)
                for e in range(3):
                    load_cb(b, e)

            def store(f):
                sp.wait_ge(s_ya, 2 * f + 2)
                sp.nop(nofuse=True)
                sp.dma_start(out_t[f], x2[:, :, :]).then_inc(s_out, 16)

            load_x_ln(0)
            sp.dma_start(wqkv_v, wqkv.rearrange("(c p) n -> p c n", p=P)).then_inc(s_wq, 16)
            sp.dma_start(wmod_v, wmod.rearrange("(c p) n -> p c n", p=P)).then_inc(s_wmod, 16)
            for dst, src in ((th[:, 0:CT * NB].rearrange("p (c b) -> p c b", c=CT),
                              cT.rearrange("(c p) b -> p c b", p=P)),
                             (ident[:, :], ident_in), (cos_s[:, :], cosT), (sin_s[:, :], sinT),
                             (gk_s[:, :, :], gk.rearrange("(c p) e -> p c e", p=P)),
                             (gb_s[:, :], gb.partition_broadcast(P)),
                             (vb_s[:, :], vb.partition_broadcast(P)),
                             (tri[:, :], tri_in.partition_broadcast(P)),
                             (qkb_s[:, :], qkb), (pb_s[:, :], pb), (pw_s[:, :, :], pw)):
                sp.dma_start(dst, src).then_inc(s_const, 16)
            stack(0, 0)
            stack(0, 1)
            iteration(0, first=True)
            with sp.Fori(1, NB - 1) as b:
                iteration(b)
            iteration(NB - 1, last=True)
            for e in range(3, E):
                load_cb(NB - 1, e)
            store(NB - 1)
            sp.wait_ge(s_out, 16 * NB)

        @block.gpsimd
        def _(pool):
            def ffn_combine(f, e):
                pool.wait_ge(s_fd, 2 * SLOTS * f + 2 * e + 1)
                if e >= E:
                    pool.nop(nofuse=True)
                if e < E:
                    pool.wait_ge(s_cb[e % 3], 16 * cb_uses[e % 3] * f + 16 * (e // 3 + 1))
                    pool.tensor_tensor(ff[:, e % 2, :], ff[:, e % 2, :], cb[:, e % 3, :],
                                       ALU.mult).then_inc(s_fp, 1)
                else:
                    pool.tensor_scalar(ff[:, e % 2, :], ff[:, e % 2, :], 0.5, None,
                                       ALU.mult).then_inc(s_fp, 1)

            def ffn_lo(f, e):
                pool.wait_ge(s_fa, 2 * SLOTS * f + 2 * e + 2)
                if e:
                    pool.wait_ge(s_dn, SLOTS * f + e)
                pool.tensor_tensor(in_lo[:, :], ff[:, e % 2, :], in_hi[:, :].bitcast(F32),
                                   ALU.subtract).then_inc(s_fp, 1)

            def rstd(n, s_ln, ve, r, s_r):
                pool.wait_ge(s_ln, LN_STEPS * n + 2 * TT + 1)
                pool.tensor_tensor(r[:, :], ve[:, :], mhalf[:, :], ALU.pow).then_inc(s_r, 1)

            def iteration(b, first=False, last=False):
                f = b - 1
                for e in range(SLOTS):
                    if first:
                        pool.wait_ge(s_whi, 2 * e + 1)
                        st = stage[e % 2]
                        pool.tensor_tensor(wgu_lo[:, e, :, :, :].rearrange("p a c m -> p (a c m)"), st[:, 0:512],
                                           wgu_hi[:, e, :, :, :].rearrange("p a c m -> p (a c m)").bitcast(F32),
                                           ALU.subtract).then_inc(s_wlo, 1)
                        pool.wait_ge(s_whi, 2 * e + 2)
                        pool.tensor_tensor(wd_lo[:, e, :], st[:, 512:768],
                                           wd_hi[:, e, :].bitcast(F32), ALU.subtract).then_inc(s_wlo, 1)
                    else:
                        ffn_combine(f, e)
                        ffn_lo(f, e)
                    if e == 9 and not last:
                        rstd(b + 1, s_ln1, ve1, rstd1, s_rstd)
                rstd(b, s_ln2, ve2, rstd2, s_rstd2)

            pool.wait_ge(s_pre, 1)
            rstd(0, s_ln1, ve1, rstd1, s_rstd)
            iteration(0, first=True)
            with pool.Fori(1, NB - 1) as b:
                iteration(b)
            iteration(NB - 1, last=True)
            for e in range(SLOTS):
                ffn_combine(NB - 1, e)
                ffn_lo(NB - 1, e)

        @block.scalar
        def _(act):
            def mod(b, k):
                return modB[:, bass.ds(b * MODS + k, 1)]

            def ffn_tanh(f, e):
                act.wait_ge(s_g, SLOTS * f + e + 1)
                if e:
                    act.wait_ge(s_fd, 2 * SLOTS * f + 2 * e - 1)
                act.activation(th[:, :], G[:, :], ACT.Tanh, scale=0.5).then_inc(s_fa, 1)

            def ffn_hi(f, e):
                act.wait_ge(s_fd, 2 * SLOTS * f + 2 * e + 2)
                if e:
                    act.wait_ge(s_dn, SLOTS * f + e)
                act.activation(in_hi[:, :], ff[:, e % 2, :], ACT.Copy).then_inc(s_fa, 1)

            def exp_group(b, g):
                for j in range(4):
                    s = 4 * g + j
                    act.wait_ge(s_st, TILES * b + s + 1)
                    if j == 0 and g >= 2:
                        act.wait_ge(s_pv, GRP * b + g - 1)
                    act.activation(pt[:, g % 2, j, :], S[s % 3][:, :], ACT.Exp, scale=SM_SCALE).then_inc(s_ex, 1)

            def copy_quad(b, quad):
                act.wait_ge(s_pv, GRP * b + 4 * quad + 4)
                if quad == 0:
                    if later(b):
                        act.wait_ge(s_pj, 2 * b)
                act.copy(on[:, quad, :], O[:, :]).then_inc(s_oc, 1)

            def h_evac(n, banks, s_ht, s_he, scale, bias):
                for c in range(CT):
                    act.wait_ge(s_ht, 2 * n + 2)
                    act.activation(hf[:, c, :], banks[c][:, :], ACT.Identity, scale=mod(n, scale + c),
                                   bias=mod(n, bias + c)).then_inc(s_he, 1)

            def y_evac(f):
                act.wait_ge(s_dn, SLOTS * (f + 1))
                act.wait_ge(s_fp, 2 * SLOTS * (f + 1))
                for c in range(CT):
                    act.activation(ff[:, c, :], Y[c][:, :], ACT.Copy, scale=mod(f, GB + c)).then_inc(s_ye, 1)

            def tail(b, first, last):
                if not last:
                    if first:
                        act.wait_ge(s_hs1, 4)
                    h_evac(b + 1, S[0:2], s_ht1, s_he1, CA, SA)
                if not first:
                    y_evac(b - 1)
                for c in range(CT):
                    act.wait_ge(s_pj, 2 * b + c + 1)
                    if not last:
                        act.wait_ge(s_hs1, 4 * b + 8)
                    act.activation((hf)[:, c, :], (G, U)[c][:, :], ACT.Identity, scale=mod(b, GA + c),
                                   bias=mod(b, GPB + c)).then_inc(s_ae, 1)
                act.wait_ge(s_at, 2 * b + 2)
                h_evac(b, S[2:4], s_ht2, s_he2, CB, SB)
                act.wait_ge(s_lg, 2 * b + 1)
                act.copy(nrm[0:E, 0, :], S[2][0:E, :]).then_inc(s_la, 1)
                act.wait_ge(s_lg, 2 * b + 2)
                if later(b):
                    act.wait_ge(s_rt, RT_STEPS * b)
                act.activation(rv[:, :, :].rearrange("p t e -> p (t e)"), S[3][:, 0:TT * E], ACT.Tanh,
                               scale=0.5).then_inc(s_la, 1)
                act.wait_ge(s_ct, b + 1)
                act.copy(nrm[0:E, 1, :], S[2][0:E, :]).then_inc(s_ce, 1)

            def iteration(b, first=False, last=False):
                f = b - 1
                for e in range(SLOTS):
                    if first:
                        act.wait_ge(s_stage[e % 2], 16 * (e // 2 + 1))
                        st = stage[e % 2]
                        act.activation(wgu_hi[:, e, :, :, :].rearrange("p a c m -> p (a c m)"), st[:, 0:512],
                                       ACT.Copy).then_inc(s_whi, 1)
                        act.activation(wd_hi[:, e, :], st[:, 512:768], ACT.Copy).then_inc(s_whi, 1)
                    else:
                        ffn_tanh(f, e)
                    gs = groups_of.get(e, ())
                    for i, g in enumerate(gs):
                        exp_group(b, g)
                        if i == 0 and not first:
                            ffn_hi(f, e)
                        if g % 4 == 0 and g > 0:
                            copy_quad(b, g // 4 - 1)
                    if not gs and not first:
                        ffn_hi(f, e)
                copy_quad(b, Q4 - 1)
                tail(b, first, last)

            act.wait_ge(s_const, 16 * CONST_DMAS)
            act.activation(nrm[:, 0, 0:CT * NB], th[:, 0:CT * NB], ACT.Tanh, scale=0.5).then_inc(s_cact, 1)
            act.wait_ge(s_pre, PRE_STEPS)
            h_evac(0, S[0:2], s_ht1, s_he1, CA, SA)
            iteration(0, first=True)
            with act.Fori(1, NB - 1) as b:
                iteration(b)
            iteration(NB - 1, last=True)
            for e in range(SLOTS):
                ffn_tanh(NB - 1, e)
                ffn_hi(NB - 1, e)
            y_evac(NB - 1)

        @block.tensor
        def _(pe):
            def split_mm(out_ap, w_hi, w_lo, x_hi, x_lo, first, last):
                pe.matmul(out_ap, w_hi, x_hi, start=first, stop=False)
                pe.matmul(out_ap, w_hi, x_lo, start=False, stop=False)
                return pe.matmul(out_ap, w_lo, upper(x_hi), start=False, stop=last)

            def gate(f, e):
                if e:
                    pe.wait_ge(s_fd, 2 * SLOTS * f + 2 * e - 1)
                else:
                    pe.wait_ge(s_ae, 2 * f + 2)
                for c in range(CT):
                    mm = split_mm(G[:, :], wgu_hi[:, e, 0, c, :], wgu_lo[:, e, 0, c, :],
                                  h_hi[:, c, :], h_lo[:, c, :], c == 0, c == CT - 1)
                mm.then_inc(s_g, 1)

            def up(f, e):
                if e:
                    pe.wait_ge(s_fd, 2 * SLOTS * f + 2 * e)
                for c in range(CT):
                    mm = split_mm(U[:, :], wgu_hi[:, e, 1, c, :], wgu_lo[:, e, 1, c, :],
                                  h_hi[:, c, :], h_lo[:, c, :], c == 0, c == CT - 1)
                mm.then_inc(s_u, 1)

            def down(f, e):
                pe.wait_ge(s_fa, 2 * SLOTS * f + 2 * e + 2)
                pe.wait_ge(s_fp, 2 * SLOTS * f + 2 * e + 2)
                for c in range(CT):
                    mm = split_mm(Y[c][:, :], wd_hi[:, e, c * P:(c + 1) * P], wd_lo[:, e, c * P:(c + 1) * P],
                                  in_hi[:, :], in_lo[:, :], e == 0, e == SLOTS - 1)
                mm.then_inc(s_dn, 1)

            def max_item(b, item):
                kind, k = item
                i = ring_at[item]
                banks = (S[0], S[1]) if i % 2 == 0 else (S[2], S[3])
                if i >= 2:
                    pe.wait_ge(s_rd, RING * b + i - 1)
                elif i == 0:
                    pe.wait_ge(s_stk, 16 * STACK_DMAS * (b + 1))
                    pe.wait_ge(s_rope, ROPE_STEPS * (b + 1))
                else:
                    if later(b):
                        pe.wait_ge(s_ce, b)
                if kind == "pair":
                    for j in range(2):
                        h, q = divmod(2 * k + j, TT)
                        mm = pe.matmul(banks[j][:, :], qs[0:ROWS, h, q * P:(q + 1) * P], ks[0:ROWS, h, :],
                                       start=True, stop=True)
                    mm.then_inc(s_smx, 1)
                else:
                    pe.wait_ge(s_mm, 4 * b + 2 * k + 2)
                    for part in range(2):
                        mm = pe.transpose(banks[0][:, :].bitcast(BF16)[0:32, part * P:(part + 1) * P],
                                          m12[:, k, part, :], ident_b[:, :])
                    mm.then_inc(s_smx, 1)

            def scores(b, g):
                quad, kt = divmod(g, TT)
                if g == 0:
                    pe.wait_ge(s_mrow, 64 * b + 64)
                    pe.wait_ge(s_rd, RING * (b + 1))
                for j in range(4):
                    s, h = 4 * g + j, 4 * quad + j
                    if s >= 3:
                        pe.wait_ge(s_ex, TILES * b + s - 2)
                    pe.matmul(S[s % 3][:, :], ks[0:ROWS + SHIFT_ROWS, h, kt * P:(kt + 1) * P],
                              qs[0:ROWS + SHIFT_ROWS, h, :], start=True, stop=True).then_inc(s_st, 1)

            def times_v(b, g):
                quad, kt = divmod(g, TT)
                pe.wait_ge(s_ex, TILES * b + 4 * g + 4)
                if g == 0:
                    pe.wait_ge(s_vb, TT * (b + 1))
                if kt == 0 and quad:
                    pe.wait_ge(s_oc, Q4 * b + quad)
                for j in range(4):
                    mm = pe.matmul(O[32 * j:32 * j + 32, :], v_s[:, kt, 4 * quad + j, :], pt[:, g % 2, j, :],
                                   start=(kt == 0), stop=(kt == TT - 1))
                mm.then_inc(s_pv, 1)

            def h_transposes(n, banks, s_ht):
                for c in range(CT):
                    for t in range(TT):
                        mm = pe.transpose(banks[c][:, t * P:(t + 1) * P], xa[:, t, c * P:(c + 1) * P], ident[:, :])
                    mm.then_inc(s_ht, 1)

            def qk(n, t):
                if t == 0:
                    pe.wait_ge(s_hs1, 4 * n + 4)
                for r in range(2):
                    col = (2 * t + r) * P
                    bank = S[(2, 0)[t] + r]
                    for c in range(CT):
                        mm = split_mm(bank[:, :], wqkv_hi[:, c, col:col + P], wqkv_lo[:, c, col:col + P],
                                      h_hi[:, c, :], h_lo[:, c, :], c == 0, c == CT - 1)
                    mm.then_inc(s_qk, 1)

            def v_proj(n):
                for t in range(TT):
                    o = Y[t // 2][:, (t % 2) * C:(t % 2 + 1) * C]
                    tok = slice(t * P, (t + 1) * P)
                    for c in range(CT):
                        pe.matmul(o, h_hi[:, c, tok], wqkv_hi[:, c, 2 * C:], start=(c == 0), stop=False)
                        pe.matmul(o, h_lo[:, c, tok], wqkv_hi[:, c, 2 * C:], start=False, stop=False)
                        mm = pe.matmul(o, upper(h_hi[:, c, tok]), wqkv_lo[:, c, 2 * C:],
                                       start=False, stop=(c == CT - 1))
                    if t % 2:
                        mm.then_inc(s_v, 1)

            def back_transposes(src, banks, s_t):
                for t in range(TT):
                    for c in range(CT):
                        o = (t % 2) * C + c * P
                        mm = pe.transpose(banks[t // 2][:, o:o + P], src[:, c, t * P:(t + 1) * P], ident[:, :])
                    if t % 2:
                        mm.then_inc(s_t, 1)

            def y_back(f):
                pe.wait_ge(s_ye, 2 * f + 2)
                back_transposes(ff, (G, U), s_yt)

            def tail(b, first, last):
                if not last:
                    pe.wait_ge(s_ln1, LN_STEPS * (b + 2))
                    pe.wait_ge(s_ex, TILES * (b + 1))
                    h_transposes(b + 1, S[0:2], s_ht1)
                if not first:
                    y_back(b - 1)
                if not last:
                    pe.wait_ge(s_oc, Q4 * b + Q4)
                    qk(b + 1, 0)
                pe.wait_ge(s_nm, NORM_STEPS * Q4 * (b + 1))
                if later(b):
                    pe.wait_ge(s_ya, 2 * b)
                for c in range(CT):
                    for quad in range(Q4):
                        mm = pe.matmul((G, U)[c][:, :], pw_s[:, quad, c * P:(c + 1) * P], on[:, quad, :],
                                       start=(quad == 0), stop=(quad == Q4 - 1))
                    mm.then_inc(s_pj, 1)
                if not last:
                    pe.wait_ge(s_he1, 2 * b + 4)
                    qk(b + 1, 1)
                    pe.wait_ge(s_rope, ROPE_STEPS * (b + 1) + 14)
                pe.wait_ge(s_ae, 2 * b + 2)
                back_transposes(hf, S[2:4], s_at)
                if not last:
                    if later(b):
                        pe.wait_ge(s_ye, 2 * b)
                    v_proj(b + 1)
                pe.wait_ge(s_ln2, LN_STEPS * (b + 1))
                h_transposes(b, S[2:4], s_ht2)
                pe.wait_ge(s_he2, 2 * b + 2)
                for c in range(CT):
                    mm = pe.matmul(S[2][0:E, :], gk_s[:, c, :], hf[:, c, :], start=(c == 0), stop=(c == CT - 1))
                mm.then_inc(s_lg, 1)
                pe.wait_ge(s_la, 2 * b + 1)
                pe.nop(nofuse=True)
                for t in range(TT):
                    mm = pe.transpose(S[3][:, t * E:(t + 1) * E], nrm[0:E, 0, t * P:(t + 1) * P], ident[0:E, 0:E])
                mm.then_inc(s_lg, 1)

            def combine_transposes(b):
                pe.wait_ge(s_rt, RT_STEPS * (b + 1))
                for t in range(TT):
                    mm = pe.transpose(S[2][0:E, t * P:(t + 1) * P], comb[:, t, :], ident[:, :])
                mm.then_inc(s_ct, 1)

            def iteration(b, first=False, last=False):
                f = b - 1
                for e in range(SLOTS):
                    items = ring_of.get(e, [])
                    gs = list(groups_of.get(e, ()))
                    if not first:
                        if e == 0:
                            pe.wait_ge(s_hs2, 4 * f + 4)
                        gate(f, e)
                    for item in items[0:2]:
                        max_item(b, item)
                    for g in gs[0:1]:
                        scores(b, g)
                        if g:
                            times_v(b, g - 1)
                    if not first:
                        up(f, e)
                        if e == 0:
                            combine_transposes(f)
                    if e >= 1 and not first:
                        if e == 1:
                            pe.wait_ge(s_vb, TT * (b + 1))
                        down(f, e - 1)
                    for item in items[2:]:
                        max_item(b, item)
                    for g in gs[1:]:
                        scores(b, g)
                        times_v(b, g - 1)
                    if e == MAX_SLOTS[-1]:
                        max_item(b, ("rows", 1))
                if not first:
                    down(f, SLOTS - 1)
                times_v(b, GRP - 1)
                tail(b, first, last)

            pe.wait_ge(s_wmod, 16)
            pe.wait_ge(s_pre, SILU_STEPS)
            for k in range(6 * CT):
                for c in range(CT):
                    mm = pe.matmul(S[2][:, k * NB:(k + 1) * NB], wmod_v[:, c, k * P:(k + 1) * P],
                                   nrm[:, 1, c * NB:(c + 1) * NB], start=(c == 0), stop=(c == CT - 1))
            mm.then_inc(s_modp, 1)
            pe.wait_ge(s_ln1, LN_STEPS)
            h_transposes(0, S[0:2], s_ht1)
            pe.wait_ge(s_pre, PRE_STEPS)
            qk(0, 0)
            pe.wait_ge(s_he1, 2)
            qk(0, 1)
            v_proj(0)
            iteration(0, first=True)
            with pe.Fori(1, NB - 1) as b:
                iteration(b)
            iteration(NB - 1, last=True)
            f = NB - 1
            pe.wait_ge(s_hs2, 4 * f + 4)
            for e in range(SLOTS):
                gate(f, e)
                up(f, e)
                if e == 0:
                    combine_transposes(f)
                else:
                    down(f, e - 1)
            down(f, SLOTS - 1)
            y_back(f)

        @block.vector
        def _(dve):
            def ffn_gated(f, e):
                dve.wait_ge(s_fa, 2 * SLOTS * f + 2 * e + 1)
                if e >= 2:
                    dve.wait_ge(s_fp, 2 * SLOTS * f + 2 * e - 2)
                dve.scalar_tensor_tensor(ff[:, e % 2, :], th[:, :], 1.0, G[:, :], ALU.add,
                                         ALU.mult).then_inc(s_fd, 1)

            def ffn_up(f, e):
                dve.wait_ge(s_u, SLOTS * f + e + 1)
                dve.wait_ge(s_fp, 2 * SLOTS * f + 2 * e + 1)
                dve.tensor_tensor(ff[:, e % 2, :], ff[:, e % 2, :], U[:, :], ALU.mult).then_inc(s_fd, 1)

            def max_item(b, item):
                kind, k = item
                i = ring_at[item]
                dve.wait_ge(s_smx, RING * b + i + 1)
                if kind == "rows":
                    src = S[0 if i % 2 == 0 else 2][:, :].bitcast(BF16)[0:32, 0:2 * P]
                    dve.tensor_copy(mT[:, k, :, :].rearrange("r a q -> r (a q)"), src).then_inc(s_rd, 1)
                    return
                lo = 0 if i % 2 == 0 else 2
                dve.tensor_reduce(mx[:, 2 * k:2 * k + 1], S[lo][:, :], AX.X, ALU.max, negate=True)
                dve.tensor_reduce(mx[:, 2 * k + 1:2 * k + 2], S[lo + 1][:, :], AX.X, ALU.max,
                                  negate=True).then_inc(s_rd, 1)
                if k in (PAIRS // 2 - 1, PAIRS - 1):
                    half = k // (PAIRS // 2)
                    m = mx[:, 32 * half:32 * half + 32]
                    dve.wait_ge(s_rd, RING * b + i + 1)
                    dve.tensor_copy(m12[:, half, 0, :], m).then_inc(s_mm, 1)
                    dve.wait_ge(s_mm, 4 * b + 2 * half + 1)
                    dve.tensor_tensor(m12[:, half, 1, :], m, m12[:, half, 0, :], ALU.subtract).then_inc(s_mm, 1)

            def norm(b, quad):
                k = NORM_STEPS * quad
                dve.wait_ge(s_oc, Q4 * b + quad + 1)
                if k or later(b):
                    dve.wait_ge(s_nm, NORM_STEPS * Q4 * b + k)
                dve.nop(nofuse=True)
                dve.stream_shuffle(nrm[:, 0, :], on[:, quad, :], [HD] * 32).then_inc(s_nm, 1)
                dve.wait_ge(s_nm, NORM_STEPS * Q4 * b + k + 1)
                dve.reciprocal(nrm[:, 1, :], nrm[:, 0, :]).then_inc(s_nm, 1)
                dve.wait_ge(s_nm, NORM_STEPS * Q4 * b + k + 2)
                dve.tensor_tensor(on[:, quad, :], on[:, quad, :], nrm[:, 1, :], ALU.mult).then_inc(s_nm, 1)

            def ln(n, src, st, mv, ve, r, s_ln, s_r):
                for t in range(TT):
                    dve.bn_stats(st[:, t, :], src[:, t, :]).then_inc(s_ln, 1)
                for t in range(TT):
                    dve.wait_ge(s_ln, LN_STEPS * n + TT)
                    dve.nop(nofuse=True)
                    dve.bn_aggr(mv[:, t, :], st[:, t, :]).then_inc(s_ln, 1)
                dve.wait_ge(s_ln, LN_STEPS * n + 2 * TT)
                dve.tensor_scalar(ve[:, :], mv[:, :, 1], LN_EPS, None, ALU.add).then_inc(s_ln, 1)
                dve.wait_ge(s_r, n + 1)
                for t in range(TT):
                    dve.tensor_scalar(xa[:, t, :], src[:, t, :], mv[:, t, 0:1], r[:, t:t + 1],
                                      ALU.subtract, ALU.mult).then_inc(s_ln, 1)

            def split_h(n, s_he, s_hs):
                for c in range(CT):
                    dve.wait_ge(s_he, 2 * n + c + 1)
                    dve.tensor_copy(h_hi[:, c, :], hf[:, c, :]).then_inc(s_hs, 1)
                for c in range(CT):
                    dve.wait_ge(s_hs, 4 * n + c + 1)
                    dve.tensor_tensor(h_lo[:, c, :], hf[:, c, :], h_hi[:, c, :].bitcast(F32),
                                      ALU.subtract).then_inc(s_hs, 1)

            def rope(n, t):
                first, second = (S[2], S[3]) if t == 0 else (S[0], S[1])
                b0, b1 = qkb_s[:, 2 * t:2 * t + 1], qkb_s[:, 2 * t + 1:2 * t + 2]
                k = 14 * t
                for r in range(2):
                    c0, c1, op = ((cos_s, sin_s, ALU.subtract), (sin_s, cos_s, ALU.add))[r]
                    dve.wait_ge(s_qk, 4 * n + 2 * t + 1)
                    if k or later(n):
                        dve.wait_ge(s_rope, ROPE_STEPS * n + k)
                    dve.scalar_tensor_tensor(rope_a, first[:, :], b0, c0[:, :], ALU.add,
                                             ALU.mult).then_inc(s_rope, 1)
                    dve.wait_ge(s_qk, 4 * n + 2 * t + 2)
                    dve.scalar_tensor_tensor(rope_b, second[:, :], b1, c1[:, :], ALU.add,
                                             ALU.mult).then_inc(s_rope, 1)
                    dve.wait_ge(s_rope, ROPE_STEPS * n + k + 2)
                    dve.tensor_tensor(rope_a, rope_a, rope_b, op).then_inc(s_rope, 1)
                    dve.wait_ge(s_rope, ROPE_STEPS * n + k + 3)
                    dve.tensor_copy(parts[t][:, 0, r, :], rope_a).then_inc(s_rope, 1)
                    dve.wait_ge(s_rope, ROPE_STEPS * n + k + 4)
                    dve.tensor_tensor(rope_a, rope_a, parts[t][:, 0, r, :], ALU.subtract).then_inc(s_rope, 1)
                    dve.wait_ge(s_rope, ROPE_STEPS * n + k + 5)
                    dve.tensor_copy(parts[t][:, 1, r, :], rope_a).then_inc(s_rope, 1)
                    dve.wait_ge(s_rope, ROPE_STEPS * n + k + 6)
                    dve.tensor_tensor(parts[t][:, 2, r, :], rope_a, parts[t][:, 1, r, :],
                                      ALU.subtract).then_inc(s_rope, 1)
                    k += 7

            def v_bias(n):
                for t in range(TT):
                    dve.wait_ge(s_v, 2 * n + t // 2 + 1)
                    dve.tensor_tensor(v_s[:, t, :, 0:HD],
                                      Y[t // 2][:, (t % 2) * C:(t % 2 + 1) * C].rearrange("p (h d) -> p h d", h=H),
                                      vb_s[:, :].rearrange("p (h d) -> p h d", h=H), ALU.add).then_inc(s_vb, 1)

            def add_y(f):
                x2f = x2[:, :, :].rearrange("p t c -> p (t c)")
                for i in range(2):
                    dve.wait_ge(s_yt, 2 * f + i + 1)
                    dve.tensor_tensor(x2f[:, i * N:(i + 1) * N], (G, U)[i][:, :], x2f[:, i * N:(i + 1) * N],
                                      ALU.add).then_inc(s_ya, 1)

            def residual(b):
                x2f = x2[:, :, :].rearrange("p t c -> p (t c)")
                xaf = xa[:, :, :].rearrange("p t c -> p (t c)")
                dve.wait_ge(s_xres, 16 * b + 16)
                if later(b):
                    dve.wait_ge(s_out, 16 * b)
                for i in range(2):
                    dve.wait_ge(s_at, 2 * b + i + 1)
                    dve.tensor_tensor(x2f[:, i * N:(i + 1) * N], S[2 + i][:, :], xaf[:, i * N:(i + 1) * N],
                                      ALU.add).then_inc(s_rs, 1)

            def router(b):
                done = 0

                def step(ins):
                    nonlocal done
                    ins.then_inc(s_rt, 1)
                    done += 1
                    dve.wait_ge(s_rt, RT_STEPS * b + done)
                    dve.nop(nofuse=True)

                dve.wait_ge(s_la, 2 * b + 2)
                step(dve.tensor_scalar(rv[:, :, :], rv[:, :, :], 0.5, 0.5, ALU.mult, ALU.add))
                step(dve.tensor_tensor(rv[:, :, :], rv[:, :, :],
                                       gb_s[:, :].unsqueeze(1).broadcast_to([P, TT, E]), ALU.add))
                v4 = rv[:, :, :].rearrange("p t (g k) -> p (t g) k", k=4)
                p2, q2 = rp, rq
                step(dve.tensor_tensor(p2, v4[:, :, 0:2], v4[:, :, 2:4], ALU.max))
                step(dve.tensor_tensor(q2, v4[:, :, 0:2], v4[:, :, 2:4], ALU.min))
                top, mid, low, gs, rank = (rs_[:, i, :] for i in range(5))
                step(dve.tensor_tensor(top, p2[:, :, 0], p2[:, :, 1], ALU.max))
                step(dve.tensor_tensor(mid, p2[:, :, 0], p2[:, :, 1], ALU.min))
                step(dve.tensor_tensor(low, q2[:, :, 0], q2[:, :, 1], ALU.max))
                step(dve.tensor_tensor(mid, mid, low, ALU.max))
                step(dve.tensor_tensor(gs, top, mid, ALU.add))
                gs3 = gs.rearrange("p (t g) -> p t g", g=4)
                other = gs3.unsqueeze(2).broadcast_to([P, TT, 4, 4])
                own = gs3.unsqueeze(3).broadcast_to([P, TT, 4, 4])
                gt = rk[:, 0, :].rearrange("p (t a b) -> p t a b", a=4, b=4)
                eq = rk[:, 1, :].rearrange("p (t a b) -> p t a b", a=4, b=4)
                step(dve.tensor_tensor(gt, other, own, ALU.is_gt))
                step(dve.tensor_tensor(eq, other, own, ALU.is_equal))
                eq2 = rk[:, 1, :].rearrange("p (t a) -> p t a", t=TT)
                step(dve.tensor_tensor(eq2, eq2, tri[:, :].unsqueeze(1).broadcast_to([P, TT, 16]), ALU.mult))
                step(dve.tensor_tensor(rk[:, 0, :], rk[:, 0, :], rk[:, 1, :], ALU.add))
                step(dve.tensor_reduce(rank, rk[:, 0, :].rearrange("p (a b) -> p a b", b=4), AX.X, ALU.add))
                step(dve.tensor_scalar(rank, rank, 1.5, None, ALU.is_lt))
                step(dve.tensor_tensor(rw[:, :, 0:E].rearrange("p t (g k) -> p t g k", k=4),
                                       rv[:, :, :].rearrange("p t (g k) -> p t g k", k=4),
                                       rank.rearrange("p (t g) -> p t g", g=4).unsqueeze(3)
                                       .broadcast_to([P, TT, 4, 4]), ALU.mult))
                step(dve.memset(rw[:, :, E:E + 4], SENTINEL))
                for t in range(TT):
                    step(dve.max(r8[:, t, :], rw[:, t, 0:E]))
                step(dve.memset(r8[:, :, 4:8], SENTINEL))
                for t in range(TT):
                    step(dve.match_replace(rr[:, t, :], r8[:, t, :], rw[:, t, :], -SENTINEL))
                step(dve.tensor_tensor(rsel[:, :, :], rr[:, :, 0:E], rw[:, :, 0:E], ALU.not_equal))
                step(dve.tensor_tensor(rsel[:, :, :], rsel[:, :, :], rw[:, :, 0:E], ALU.mult))
                step(dve.tensor_reduce(rsum[:, 0, :], rsel[:, :, :], AX.X, ALU.add))
                step(dve.tensor_scalar(rsum[:, 1, :], rsum[:, 0, :], TOPK_EPS, None, ALU.add))
                step(dve.reciprocal(rsum[:, 2, :], rsum[:, 1, :]))
                step(dve.scalar_tensor_tensor(comb[:, :, :], rsel[:, :, :], 0.5 * ROUTE_SCALE,
                                              rsum[:, 2, :].unsqueeze(2).broadcast_to([P, TT, E]),
                                              ALU.mult, ALU.mult))
                assert done == RT_STEPS, done

            def tail(b, first, last):
                if not last:
                    split_h(b + 1, s_he1, s_hs1)
                if not first:
                    add_y(b - 1)
                norm(b, Q4 - 1)
                if not last:
                    rope(b + 1, 0)
                if first:
                    dve.wait_ge(s_wlo, 2 * SLOTS)
                residual(b)
                dve.wait_ge(s_rs, 2 * b + 2)
                ln(b, x2, st2, mv2, ve2, rstd2, s_ln2, s_rstd2)
                if not last:
                    v_bias(b + 1)
                split_h(b, s_he2, s_hs2)
                if not last:
                    rope(b + 1, 1)
                router(b)

            def iteration(b, first=False, last=False):
                f = b - 1
                for e in range(SLOTS):
                    items = ring_of.get(e, [])
                    if not first:
                        ffn_gated(f, e)
                    for item in items[0:2]:
                        max_item(b, item)
                    if not first:
                        ffn_up(f, e)
                    for item in items[2:]:
                        max_item(b, item)
                    if e == MAX_SLOTS[-1]:
                        max_item(b, ("rows", 1))
                    if e == 9 and not last:
                        dve.wait_ge(s_xln, 16 * b + 32)
                        ln(b + 1, xa, st1, mv1, ve1, rstd1, s_ln1, s_rstd)
                    gs = list(groups_of.get(e, ()))
                    for g in gs:
                        if g % 4 == 2 and g > 4:
                            norm(b, g // 4 - 1)
                tail(b, first, last)

            pre = [0]

            def step(ins):
                ins.then_inc(s_pre, 1)
                pre[0] += 1
                dve.wait_ge(s_pre, pre[0])

            step(dve.memset(mhalf[:, :], -0.5))
            step(dve.memset(ks[ROWS:ROWS + SHIFT_ROWS, :, :], 1.0))
            step(dve.memset(v_s[:, :, :, HD:32], 1.0))
            dve.wait_ge(s_const, 16 * CONST_DMAS)
            step(dve.tensor_copy(ident_b[:, :], ident[:, :]))
            dve.wait_ge(s_cact, 1)
            ctb = th[:, 0:CT * NB]
            step(dve.tensor_scalar(nrm[:, 0, 0:CT * NB], nrm[:, 0, 0:CT * NB], 0.5, 0.5, ALU.mult, ALU.add))
            step(dve.tensor_tensor(nrm[:, 1, 0:CT * NB], nrm[:, 0, 0:CT * NB], ctb, ALU.mult))
            assert pre[0] == SILU_STEPS
            dve.wait_ge(s_xln, 16)
            ln(0, xa, st1, mv1, ve1, rstd1, s_ln1, s_rstd)
            dve.wait_ge(s_wq, 16)
            step(dve.tensor_copy(wqkv_hi[:, :, :], wqkv_v))
            step(dve.tensor_tensor(wqkv_lo[:, :, :], wqkv_v, wqkv_hi[:, :, :].bitcast(F32), ALU.subtract))
            dve.wait_ge(s_modp, 1)
            mp = S[2][:, 0:6 * CT * NB].rearrange("p (k b) -> p b k", b=NB)
            tab = modB[:, :].rearrange("p (b k) -> p b k", k=MODS)
            for chunk, (dst, plus) in enumerate(((SA, 0.0), (CA, 1.0), (GA, 0.0), (SB, 0.0), (CB, 1.0), (GB, 0.0))):
                step(dve.tensor_scalar(tab[:, :, dst:dst + 2], mp[:, :, 2 * chunk:2 * chunk + 2], plus, None,
                                       ALU.add))
            for dst in (GA, GB):
                g = tab[:, :, dst:dst + 2]
                mag = nrm[:, 0, 0:2 * NB].rearrange("p (b k) -> p b k", k=2)
                sgn = nrm[:, 0, 2 * NB:4 * NB].rearrange("p (b k) -> p b k", k=2)
                step(dve.scalar_tensor_tensor(mag, g, -1.0, g, ALU.mult, ALU.max))
                step(dve.tensor_scalar(mag, mag, GATE_MIN, None, ALU.max))
                step(dve.tensor_scalar(sgn, g, 0.0, 2.0, ALU.is_ge, ALU.mult))
                step(dve.tensor_scalar(sgn, sgn, 1.0, None, ALU.subtract))
                step(dve.tensor_tensor(g, mag, sgn, ALU.mult))
            step(dve.tensor_tensor(tab[:, :, GPB:GPB + 2], tab[:, :, GA:GA + 2],
                                   pb_s[:, :].unsqueeze(1).broadcast_to([P, NB, 2]), ALU.mult))
            assert pre[0] == PRE_STEPS, pre[0]
            split_h(0, s_he1, s_hs1)
            rope(0, 0)
            rope(0, 1)
            v_bias(0)
            iteration(0, first=True)
            with dve.Fori(1, NB - 1) as b:
                iteration(b)
            iteration(NB - 1, last=True)
            for e in range(SLOTS):
                ffn_gated(NB - 1, e)
                ffn_up(NB - 1, e)
            add_y(NB - 1)


SILU_STEPS = 6
PRE_STEPS = SILU_STEPS + 2 + 6 + 10 + 1


def layouts(a):
    f32 = np.float32
    qkv = a["L0_attn_qkv_w"]
    wqk = qkv[:2 * C].reshape(2, H, HALF, 2, C).transpose(4, 0, 3, 2, 1).reshape(C, 2 * C)
    wqkv = np.concatenate([wqk, qkv[2 * C:].T], axis=1)
    qkb = a["L0_attn_qkv_b"][:2 * C].reshape(2, H, HALF, 2).transpose(2, 1, 0, 3).reshape(P, 4)
    pw = np.zeros((4, 32, Q4, C), f32)
    pw[:, :HD] = a["L0_attn_proj_w"].T.reshape(Q4, 4, HD, C).transpose(1, 2, 0, 3)
    def cols(w):
        return w.reshape(C, 2, M).transpose(1, 0, 2)
    gate = np.concatenate([a["L0_ffn_w_gate"], cols(a["L0_ffn_sw_gate"])])
    up = np.concatenate([a["L0_ffn_w_up"], cols(a["L0_ffn_sw_up"])])
    gu = np.stack([gate, up], 1).reshape(SLOTS, 2, CT, P, M).transpose(0, 3, 1, 2, 4).reshape(SLOTS, P, 4 * M)
    down = np.concatenate([a["L0_ffn_w_down"], a["L0_ffn_sw_down"].reshape(2, M, C)])
    inv = f32(1.0) / f32(10000.0) ** (np.arange(0, HD, 2, dtype=f32) / f32(HD))
    freqs = np.arange(N, dtype=f32)[None, :] * np.repeat(inv, H)[:, None]
    tri = (np.arange(4)[None, :] < np.arange(4)[:, None]).astype(f32).reshape(16)
    return {
        "x": a["L0_attn_x"], "cT": a["L0_c"].T, "wmod": a["L0_wmod"], "wqkv": wqkv, "qkb": qkb,
        "vb": a["L0_attn_qkv_b"][2 * C:], "pw": pw.reshape(P, Q4, C),
        "pb": a["L0_attn_proj_b"].reshape(CT, P).T, "gk": a["L0_ffn_gate_kernel"],
        "gb": a["L0_ffn_gate_bias"], "wffn": np.concatenate([gu, down], axis=2),
        "cosT": np.cos(freqs), "sinT": np.sin(freqs), "ident_in": np.eye(P, dtype=f32), "tri_in": tri,
    }


def kernel(**inputs):
    import concourse.bacc as bacc
    from concourse.bass_utils import run_bass_kernel_spmd

    nc = bacc.Bacc("TRN2", target_bir_lowering=False, num_devices=1)
    arrays = {k: np.ascontiguousarray(v) for k, v in layouts({k: np.asarray(v) for k, v in inputs.items()}).items()}
    args = {k: nc.dram_tensor(k, v.shape, F32, kind="ExternalInput").ap() for k, v in arrays.items()}
    out = nc.dram_tensor("out", (NB, N, C), F32, kind="ExternalOutput").ap()
    build(nc, **args, out=out)
    r = run_bass_kernel_spmd(nc, [arrays], core_ids=[0])
    return r.results[0]["out"]
```

```python
from contextlib import ExitStack

import numpy as np

import concourse.bass as bass
from concourse import mybir

F32 = mybir.dt.float32
F32R = mybir.dt.float32r
BF16 = mybir.dt.bfloat16
ALU = mybir.AluOpType
ACT = mybir.ActivationFunctionType
AX = mybir.AxisListType

P = 128
NB, N, C = 16, 512, 256
H, HD = 16, 16
HALF = HD // 2
E, M = 16, 128
SLOTS = E + 2
TT = N // P
CT = C // P
Q4 = H // 4
LN_EPS = 1e-5
TOPK_EPS = 1e-20
ROUTE_SCALE = 2.5
GATE_MIN = 0.25
SM_SCALE = float(HD) ** -0.5
CONST_DMAS = 11
SENTINEL = -3.0e38

Q_PART = (0, 0, 1, 1, 0, 2)
K_PART = (0, 1, 0, 1, 2, 0)
GROUPS = len(Q_PART)
ROWS = GROUPS * HD
SHIFT_ROWS = 2

SA, CA, GA, GPB, SB, CB, GB = range(0, 14, 2)
MODS = 14

PAIRS = H * TT // 2
RING = PAIRS + 2
TILES = H * TT
GRP = TILES // 4
LN_STEPS = 3 * TT + 1
ROPE_STEPS = 12
PART_STEPS = 8
NORM_STEPS = 4
RT_STEPS = 32
STACK_DMAS = 2 * 2 * GROUPS
SHARED = SLOTS - E
MAX_ITEMS = (0, 5, 5, 4, 4, 4, 4, 4, 4)
EXP_GROUPS = {9: 4, 10: 3, 11: 3, 12: 3, 13: 3}
VW = HD + 1


def build(nc, x, cT, wmod, wqkv, qkb, vb, pw, pb, gk, gb, wffn, cosT, sinT, ident_in, tri_in, out):
    ctx = ExitStack()
    with ctx:
        def sb(name, shape, dt=F32):
            return ctx.enter_context(nc.sbuf_tensor(name, shape, dt))

        def sem(name):
            return ctx.enter_context(nc.semaphore(name))

        wgu_hi = sb("wgu_hi", [P, SLOTS, 2, CT, M], F32R)
        wgu_lo = sb("wgu_lo", [P, SLOTS, 2, CT, M], BF16)
        wd_hi = sb("wd_hi", [P, SLOTS, C], F32R)
        wd_lo = sb("wd_lo", [P, SLOTS, C], BF16)
        wqkv_hi = sb("wqkv_hi", [P, CT, 3 * C], F32R)
        wqkv_lo = sb("wqkv_lo", [P, CT, 3 * C], BF16)
        pw_s = sb("pw_s", [P, Q4, C])
        cos_s = sb("cos_s", [P, N])
        sin_s = sb("sin_s", [P, N])
        ident = sb("ident", [P, P])
        ident_b = sb("ident_b", [P, P], BF16)
        gk_s = sb("gk_s", [P, CT, E])
        gb_s = sb("gb_s", [P, E])
        vb_s = sb("vb_s", [P, C])
        qkb_s = sb("qkb_s", [P, 4])
        pb_s = sb("pb_s", [P, CT])
        tri = sb("tri", [P, 16])
        mhalf = sb("mhalf", [P, TT])
        modB = sb("modB", [P, NB * MODS])

        qs = sb("qs", [P, H, N], BF16)
        ks = sb("ks", [P, H, N], BF16)
        pt = sb("pt", [P, 2, 4, N])
        v_s = sb("v_s", [P, TT, H * VW + 32 - VW + 1])
        h1_hi = sb("h1_hi", [P, CT, N], F32R)
        h1_lo = sb("h1_lo", [P, CT, N], F32R)
        on = sb("on", [P, Q4, N])
        nrm = sb("nrm", [P, N])
        rec = sb("rec", [P, N // 32])
        xa = sb("xa", [P, TT, C])
        x2 = sb("x2", [P, TT, C])
        hf = sb("hf", [P, CT, N])
        h_hi = sb("h_hi", [P, CT, N], F32R)
        h_lo = sb("h_lo", [P, CT, N], F32R)
        cb = sb("cb", [P, 3, N])
        ff = sb("ff", [P, 2, N])
        in_hi = sb("in_hi", [P, N], F32R)
        in_lo = sb("in_lo", [P, N], F32R)
        mx = sb("mx", [P, TILES])
        m12 = sb("m12", [P, 2, 2, 32], BF16)
        mT = sb("mT", [32, 2, 2, P], BF16)
        st1, st2 = sb("st1", [P, TT, 6]), sb("st2", [P, TT, 6])
        mv1, mv2 = sb("mv1", [P, TT, 2]), sb("mv2", [P, TT, 2])
        ve1, ve2 = sb("ve1", [P, TT]), sb("ve2", [P, TT])
        rstd1, rstd2 = sb("rstd1", [P, TT]), sb("rstd2", [P, TT])
        rv = sb("rv", [P, TT, E])

        cd = nc.dram_tensor("combine_rows", [E, N], F32, kind="Internal").ap()

        S4 = ctx.enter_context(nc.psum_tensor("S4", [P, 4, N], F32))
        S = [S4[:, i, :] for i in range(4)]
        G = ctx.enter_context(nc.psum_tensor("G", [P, N], F32))
        U = ctx.enter_context(nc.psum_tensor("U", [P, N], F32))
        Y = [ctx.enter_context(nc.psum_tensor(f"Y{i}", [P, N], F32)) for i in range(2)]
        O = S[3]

        wmod_v = qs[:, :, :].rearrange("p h n -> p (h n)").bitcast(F32)[:, 0:CT * 6 * C] \
            .rearrange("p (c n) -> p c n", c=CT)
        ptf = pt[:, :, :, :].rearrange("p a b n -> p (a b) n")
        wqkv_v = pt[:, :, :, :].rearrange("p a b n -> p (a b n)")[:, 0:CT * 3 * C] \
            .rearrange("p (c n) -> p c n", c=CT)
        parts = [ptf[:, 3 * t:3 * t + 3, :].rearrange("p a n -> p (a n)").bitcast(BF16)
                 .rearrange("p (j r n) -> p j r n", j=3, r=2) for t in range(2)]
        rope_a, rope_b = (ptf[:, 6, :], ptf[:, 7, :]), nrm[:, :]
        v_heads = [v_s[:, t, 0:H * VW].rearrange("p (h d) -> p h d", h=H) for t in range(TT)]
        scratch = on[:, :, :].rearrange("p q n -> p (q n)")
        at = [0]

        def cut(*shape):
            n = int(np.prod(shape))
            v = scratch[:, at[0]:at[0] + n]
            at[0] += n
            names = "abc"[:len(shape)]
            return v.rearrange(f"p ({' '.join(names)}) -> p {' '.join(names)}",
                               **dict(zip(names[1:], shape[1:]))) if len(shape) > 1 else v

        rp, rq = cut(4 * TT, 2), cut(4 * TT, 2)
        rs_ = cut(5, 4 * TT)
        rk = cut(2, 16 * TT)
        rw, rr = cut(TT, E + 4), cut(TT, E + 4)
        r8 = cut(TT, 8)
        rsel = cut(TT, E)
        rsum = cut(3, TT)
        comb = cut(TT, E)
        c_raw = hf[:, 0, 0:CT * NB]
        c_tanh, c_silu = nrm[:, 0:CT * NB], nrm[:, CT * NB:2 * CT * NB]
        gate_mag, gate_sgn = nrm[:, 2 * CT * NB:2 * CT * NB + 2 * NB], nrm[:, 2 * CT * NB + 2 * NB:2 * CT * NB + 4 * NB]
        hft = hf[:, :, :].rearrange("p c n -> p (c n)").rearrange("p (t c) -> p t c", t=TT)
        stage = [x2[:, :, :].rearrange("p t c -> p (t c)"), ff[:, :, :].rearrange("p a n -> p (a n)")]

        def upper(ap):
            return ap.bitcast(BF16)[:, 1::2]

        s_const = sem("s_const")
        s_wmod, s_wq, s_x0 = sem("s_wmod"), sem("s_wq"), sem("s_x0")
        s_pre = sem("s_pre")
        s_cact = sem("s_cact")
        s_modp = sem("s_modp")
        s_stage = [sem("s_stage0"), sem("s_stage1")]
        s_whi = sem("s_whi")
        s_wlo = sem("s_wlo")
        s_xln = sem("s_xln")
        s_xres = sem("s_xres")
        s_ln1, s_ln2 = sem("s_ln1"), sem("s_ln2")
        s_rstd1, s_rstd2 = sem("s_rstd1"), sem("s_rstd2")
        s_ht1, s_ht2 = sem("s_ht1"), sem("s_ht2")
        s_he1, s_he2 = sem("s_he1"), sem("s_he2")
        s_hs1, s_hs2 = sem("s_hs1"), sem("s_hs2")
        s_qk = sem("s_qk")
        s_v = sem("s_v")
        s_vb = sem("s_vb")
        s_rope = sem("s_rope")
        s_pa = sem("s_pa")
        s_pp = sem("s_pp")
        s_stk = sem("s_stk")
        s_smx = sem("s_smx")
        s_rd = sem("s_rd")
        s_mm = sem("s_mm")
        s_mrow = [sem("s_mrow0"), sem("s_mrow1")]
        s_st = sem("s_st")
        s_ex = sem("s_ex")
        s_pv = sem("s_pv")
        s_nm = sem("s_nm")
        s_pj = sem("s_pj")
        s_ae = sem("s_ae")
        s_at = sem("s_at")
        s_rs = sem("s_rs")
        s_lg = sem("s_lg")
        s_la = sem("s_la")
        s_rt = sem("s_rt")
        s_ct = sem("s_ct")
        s_ce = sem("s_ce")
        s_cdw = sem("s_cdw")
        s_cb = [sem(f"s_cb{i}") for i in range(3)]
        cb_uses = [len(range(i, E, 3)) for i in range(3)]
        s_g, s_u = sem("s_g"), sem("s_u")
        s_fa = sem("s_fa")
        s_fd = sem("s_fd")
        s_fp = sem("s_fp")
        s_dn = sem("s_dn")
        s_ye = sem("s_ye")
        s_yt = sem("s_yt")
        s_ya = sem("s_ya")
        s_out = sem("s_out")
        s_x2 = sem("s_x2")

        def later(b):
            return not isinstance(b, int) or b > 0

        x_t = x.rearrange("b (t p) c -> b p t c", p=P)
        out_t = out.rearrange("b (t p) c -> b p t c", p=P)

        ring = [("pair", p) for p in range(18)] + [("rows", 0)] + [("pair", p) for p in range(18, PAIRS)] \
            + [("rows", 1)]
        ring_at = {item: i for i, item in enumerate(ring)}
        ring_of, groups_of = {}, {}
        start = 0
        for e, items in enumerate(MAX_ITEMS):
            ring_of[e] = ring[start:start + items]
            start += items
        assert start == len(ring) == RING
        start = 0
        for e, groups in EXP_GROUPS.items():
            groups_of[e] = list(range(start, start + groups))
            start += groups
        assert start == GRP
        rows_slot = [next(e for e in ring_of if ("rows", k) in ring_of[e]) for k in range(2)]

        block = ctx.enter_context(nc.Block())

        @block.sync
        def _(sp):
            def load_cb(f, x):
                if x < 3:
                    last = max(k for k in range(E) if k % 3 == x)
                    if later(f):
                        sp.wait_ge(s_fp, 2 * SLOTS * (f - 1) + 2 * (SHARED + last) + 1)
                else:
                    sp.wait_ge(s_fp, 2 * SLOTS * f + 2 * (SHARED + x - 3) + 1)
                sp.dma_start(cb[:, x % 3, :], cd[x, :].partition_broadcast(P)).then_inc(s_cb[x % 3], 16)

            def shift_rows(b, half):
                sp.wait_ge(s_rd, RING * b + ring_at[("rows", half)] + 1)
                for part in range(SHIFT_ROWS):
                    dst = qs[ROWS + part:ROWS + part + 1, half * 8:half * 8 + 8, :] \
                        .rearrange("o h n -> o (h n)").rearrange("o (r q) -> o r q", q=P)
                    sp.dma_start(dst, mT[:, half, part, :]).then_inc(s_mrow[half], 16)

            def stack(n, t):
                for r in range(2):
                    sp.wait_ge(s_pp, PART_STEPS * n + 4 * t + 3 + r)
                    for g in range(GROUPS):
                        row = g * HD + r * HALF
                        dst = (qs, ks)[t][row:row + HALF, :, :]
                        src = parts[t][:, (Q_PART, K_PART)[t][g], r, :]
                        sp.dma_start(dst, src).then_inc(s_stk, 16)

            def load_x_ln(b, first):
                if first:
                    sp.wait_ge(s_ht1, 2)
                else:
                    sp.wait_ge(s_x2, 16 * b)
                    sp.nop(nofuse=True)
                sp.dma_start(xa[:, :, :], x_t[b + 1]).then_inc(s_xln, 16)

            def load_x_res(b, last):
                if last:
                    sp.wait_ge(s_x2, 16 * b)
                    sp.nop(nofuse=True)
                else:
                    sp.wait_ge(s_ht1, 2 * b + 4)
                    sp.nop(nofuse=True)
                sp.dma_start(xa[:, :, :], x_t[b]).then_inc(s_xres, 16)

            def store(f):
                sp.wait_ge(s_ya, 2 * f + 2)
                sp.nop(nofuse=True)
                sp.dma_start(out_t[f], x2[:, :, :]).then_inc(s_out, 16)

            def keep_residual(b, first):
                if first:
                    sp.wait_ge(s_wlo, 2 * SLOTS)
                else:
                    sp.wait_ge(s_out, 16 * b)
                    sp.nop(nofuse=True)
                sp.wait_ge(s_rs, 2 * b + 2)
                sp.dma_start(x2[:, :, :], xa[:, :, :]).then_inc(s_x2, 16)

            def combine_rows(b):
                sp.wait_ge(s_ce, b + 1)
                sp.nop(nofuse=True)
                for i in range(3):
                    if later(b):
                        sp.wait_ge(s_cb[i], 16 * cb_uses[i] * b)
                        sp.nop(nofuse=True)
                sp.dma_start(cd, nrm[0:E, :]).then_inc(s_cdw, 16)
                sp.wait_ge(s_cdw, 16 * b + 16)
                sp.nop(nofuse=True)
                for x in range(3):
                    load_cb(b, x)

            def iteration(b, first=False, last=False):
                f = b - 1
                for e in range(SLOTS):
                    if e == rows_slot[0] + 1:
                        shift_rows(b, 0)
                    if e == rows_slot[1] + 1:
                        shift_rows(b, 1)
                    if first:
                        if e >= 2:
                            sp.wait_ge(s_wlo, 2 * (e - 1))
                        sp.dma_start(stage[e % 2][:, 0:768], wffn[e]).then_inc(s_stage[e % 2], 16)
                    elif 3 <= e + 1 < E:
                        load_cb(f, e + 1)
                    if e == 3 and not last:
                        load_x_ln(b, first)
                    if e == rows_slot[1] + 1:
                        load_x_res(b, last)
                    if e == 14 and not last:
                        stack(b + 1, 0)
                    if e == 16 and not last:
                        stack(b + 1, 1)
                if not first:
                    store(f)
                keep_residual(b, first)
                combine_rows(b)

            sp.dma_start(xa[:, :, :], x_t[0]).then_inc(s_xln, 16)
            sp.dma_start(wqkv_v, wqkv.rearrange("(c p) n -> p c n", p=P)).then_inc(s_wq, 16)
            sp.dma_start(wmod_v, wmod.rearrange("(c p) n -> p c n", p=P)).then_inc(s_wmod, 16)
            for dst, src in ((c_raw.rearrange("p (c b) -> p c b", c=CT), cT.rearrange("(c p) b -> p c b", p=P)),
                             (ident[:, :], ident_in), (cos_s[:, :], cosT), (sin_s[:, :], sinT),
                             (gk_s[:, :, :], gk.rearrange("(c p) e -> p c e", p=P)),
                             (gb_s[:, :], gb.partition_broadcast(P)),
                             (vb_s[:, :], vb.partition_broadcast(P)),
                             (tri[:, :], tri_in.partition_broadcast(P)),
                             (qkb_s[:, :], qkb), (pb_s[:, :], pb), (pw_s[:, :, :], pw)):
                sp.dma_start(dst, src).then_inc(s_const, 16)
            stack(0, 0)
            stack(0, 1)
            iteration(0, first=True)
            with sp.Fori(1, NB - 1) as b:
                iteration(b)
            iteration(NB - 1, last=True)
            for x in range(3, E):
                load_cb(NB - 1, x)
            store(NB - 1)
            sp.wait_ge(s_out, 16 * NB)

        @block.gpsimd
        def _(pool):
            def combine(f, e):
                pool.wait_ge(s_fd, 2 * SLOTS * f + 2 * e + 1)
                if e < SHARED:
                    pool.nop(nofuse=True)
                    pool.tensor_scalar(ff[:, e % 2, :], ff[:, e % 2, :], 0.5, None,
                                       ALU.mult).then_inc(s_fp, 1)
                else:
                    x = e - SHARED
                    pool.wait_ge(s_cb[x % 3], 16 * cb_uses[x % 3] * f + 16 * (x // 3 + 1))
                    pool.tensor_tensor(ff[:, e % 2, :], ff[:, e % 2, :], cb[:, x % 3, :],
                                       ALU.mult).then_inc(s_fp, 1)

            def in_low(f, e):
                pool.wait_ge(s_fa, 2 * SLOTS * f + 2 * e + 2)
                if e:
                    pool.wait_ge(s_dn, SLOTS * f + e)
                pool.tensor_tensor(in_lo[:, :], ff[:, e % 2, :], in_hi[:, :].bitcast(F32),
                                   ALU.subtract).then_inc(s_fp, 1)

            def remainders(n, t, which):
                for r in range(2):
                    k = PART_STEPS * n + 4 * t + 2 * which + r
                    pool.wait_ge(s_pa, k + 1)
                    dst = rope_a[r] if which == 0 else parts[t][:, 2, r, :]
                    pool.tensor_tensor(dst, rope_a[r], parts[t][:, which, r, :], ALU.subtract).then_inc(s_pp, 1)

            def rstd(n, s_ln, ve, r, s_r):
                pool.wait_ge(s_ln, LN_STEPS * n + 2 * TT + 1)
                pool.tensor_tensor(r[:, :], ve[:, :], mhalf[:, :], ALU.pow).then_inc(s_r, 1)

            def weights_lo(e):
                pool.wait_ge(s_whi, 2 * e + 1)
                st = stage[e % 2]
                pool.tensor_tensor(wgu_lo[:, e, :, :, :].rearrange("p a c m -> p (a c m)"), st[:, 0:512],
                                   wgu_hi[:, e, :, :, :].rearrange("p a c m -> p (a c m)").bitcast(F32),
                                   ALU.subtract).then_inc(s_wlo, 1)
                pool.wait_ge(s_whi, 2 * e + 2)
                pool.tensor_tensor(wd_lo[:, e, :], st[:, 512:768],
                                   wd_hi[:, e, :].bitcast(F32), ALU.subtract).then_inc(s_wlo, 1)

            def iteration(b, first=False, last=False):
                f = b - 1
                for e in range(SLOTS):
                    if first:
                        weights_lo(e)
                    else:
                        combine(f, e)
                    if not last:
                        if e == 7:
                            rstd(b + 1, s_ln1, ve1, rstd1, s_rstd1)
                        if e == 14:
                            remainders(b + 1, 0, 0)
                        if e == 16:
                            remainders(b + 1, 1, 1)
                    if not first:
                        in_low(f, e)
                    if not last:
                        if e == 14:
                            remainders(b + 1, 0, 1)
                        if e == 15:
                            remainders(b + 1, 1, 0)
                    if e == 15:
                        rstd(b, s_ln2, ve2, rstd2, s_rstd2)

            pool.wait_ge(s_pre, 1)
            rstd(0, s_ln1, ve1, rstd1, s_rstd1)
            for t in range(2):
                remainders(0, t, 0)
                remainders(0, t, 1)
            iteration(0, first=True)
            with pool.Fori(1, NB - 1) as b:
                iteration(b)
            iteration(NB - 1, last=True)
            for e in range(SLOTS):
                combine(NB - 1, e)
                in_low(NB - 1, e)

        @block.scalar
        def _(act):
            def mod(b, k):
                return modB[:, bass.ds(b * MODS + k, 1)]

            def gate_tanh(f, e):
                act.wait_ge(s_g, SLOTS * f + e + 1)
                if e >= 2:
                    act.wait_ge(s_fp, 2 * SLOTS * f + 2 * e - 2)
                act.activation(ff[:, e % 2, :], G[:, :], ACT.Tanh, scale=0.5).then_inc(s_fa, 1)

            def in_high(f, e):
                act.wait_ge(s_fd, 2 * SLOTS * f + 2 * e + 2)
                if e:
                    act.wait_ge(s_dn, SLOTS * f + e)
                act.activation(in_hi[:, :], ff[:, e % 2, :], ACT.Copy).then_inc(s_fa, 1)

            def exp_group(b, g):
                for j in range(4):
                    s = 4 * g + j
                    act.wait_ge(s_st, TILES * b + s + 1)
                    if j == 0 and g >= 2:
                        act.wait_ge(s_pv, GRP * b + g - 1)
                    act.activation(pt[:, g % 2, j, :], S[s % 3], ACT.Exp, scale=SM_SCALE).then_inc(s_ex, 1)

            def h_evac(n, banks, s_ht, s_he, scale, bias):
                for c in range(CT):
                    act.wait_ge(s_ht, 2 * n + 2)
                    act.activation(hf[:, c, :], banks[c], ACT.Identity, scale=mod(n, scale + c),
                                   bias=mod(n, bias + c)).then_inc(s_he, 1)

            def part_copies(n, t, which):
                for r in range(2):
                    if which == 0:
                        act.wait_ge(s_rope, ROPE_STEPS * n + 6 * t + 3 * (r + 1))
                    else:
                        act.wait_ge(s_pp, PART_STEPS * n + 4 * t + r + 1)
                    act.activation(parts[t][:, which, r, :], rope_a[r], ACT.Copy).then_inc(s_pa, 1)

            def proj_evac(b):
                for c in range(CT):
                    act.wait_ge(s_pj, 2 * b + c + 1)
                    act.activation(hf[:, c, :], S[2 + c], ACT.Identity, scale=mod(b, GA + c),
                                   bias=mod(b, GPB + c)).then_inc(s_ae, 1)

            def logits_copy(b):
                act.wait_ge(s_lg, 2 * b + 1)
                act.copy(nrm[0:E, :], S[2][0:E, :]).then_inc(s_la, 1)

            def router_tanh(b):
                act.wait_ge(s_lg, 2 * b + 2)
                if later(b):
                    act.wait_ge(s_rt, RT_STEPS * b)
                act.activation(rv[:, :, :].rearrange("p t e -> p (t e)"), S[3][:, 0:TT * E], ACT.Tanh,
                               scale=0.5).then_inc(s_la, 1)

            def combine_copy(f):
                act.wait_ge(s_ct, f + 1)
                act.copy(nrm[0:E, :], S[0][0:E, :]).then_inc(s_ce, 1)

            def y_evac(f):
                act.wait_ge(s_dn, SLOTS * (f + 1))
                act.wait_ge(s_fp, 2 * SLOTS * (f + 1))
                for c in range(CT):
                    act.activation(ff[:, c, :], Y[c][:, :], ACT.Copy, scale=mod(f, GB + c)).then_inc(s_ye, 1)

            def weights_hi(e):
                act.wait_ge(s_stage[e % 2], 16 * (e // 2 + 1))
                st = stage[e % 2]
                act.activation(wgu_hi[:, e, :, :, :].rearrange("p a c m -> p (a c m)"), st[:, 0:512],
                               ACT.Copy).then_inc(s_whi, 1)
                act.activation(wd_hi[:, e, :], st[:, 512:768], ACT.Copy).then_inc(s_whi, 1)

            def iteration(b, first=False, last=False):
                f = b - 1
                for e in range(SLOTS):
                    if e == 9 and not last:
                        h_evac(b + 1, S[0:2], s_ht1, s_he1, CA, SA)
                    if first:
                        weights_hi(e)
                    else:
                        gate_tanh(f, e)
                        if e == 0:
                            combine_copy(f)
                    gs = groups_of.get(e, [])
                    for g in gs[0:1]:
                        exp_group(b, g)
                    if e == 14 and not last:
                        part_copies(b + 1, 0, 0)
                    if e == 16 and not last:
                        part_copies(b + 1, 1, 1)
                    if e == 17:
                        logits_copy(b)
                    if not first:
                        in_high(f, e)
                    for g in gs[1:]:
                        exp_group(b, g)
                    if e == 14:
                        if not last:
                            part_copies(b + 1, 0, 1)
                        proj_evac(b)
                    if e == 15 and not last:
                        part_copies(b + 1, 1, 0)
                    if e == 16:
                        h_evac(b, S[2:4], s_ht2, s_he2, CB, SB)
                    if e == 17:
                        router_tanh(b)
                if not first:
                    y_evac(f)

            act.wait_ge(s_const, 16 * CONST_DMAS)
            act.activation(c_tanh, c_raw, ACT.Tanh, scale=0.5).then_inc(s_cact, 1)
            act.wait_ge(s_pre, PRE_STEPS)
            h_evac(0, S[0:2], s_ht1, s_he1, CA, SA)
            for t in range(2):
                part_copies(0, t, 0)
                part_copies(0, t, 1)
            iteration(0, first=True)
            with act.Fori(1, NB - 1) as b:
                iteration(b)
            iteration(NB - 1, last=True)
            for e in range(SLOTS):
                gate_tanh(NB - 1, e)
                if e == 0:
                    combine_copy(NB - 1)
                in_high(NB - 1, e)
            y_evac(NB - 1)

        @block.tensor
        def _(pe):
            def split_mm(out_ap, w_hi, w_lo, x_hi, x_lo, first, last):
                pe.matmul(out_ap, w_hi, x_hi, start=first, stop=False)
                pe.matmul(out_ap, w_hi, x_lo, start=False, stop=False)
                return pe.matmul(out_ap, w_lo, upper(x_hi), start=False, stop=last)

            def gate(f, e):
                if e:
                    pe.wait_ge(s_fd, 2 * SLOTS * f + 2 * e - 1)
                else:
                    pe.wait_ge(s_hs2, 4 * f + 4)
                for c in range(CT):
                    mm = split_mm(G[:, :], wgu_hi[:, e, 0, c, :], wgu_lo[:, e, 0, c, :],
                                  h_hi[:, c, :], h_lo[:, c, :], c == 0, c == CT - 1)
                mm.then_inc(s_g, 1)

            def up(f, e):
                if e:
                    pe.wait_ge(s_fd, 2 * SLOTS * f + 2 * e)
                for c in range(CT):
                    mm = split_mm(U[:, :], wgu_hi[:, e, 1, c, :], wgu_lo[:, e, 1, c, :],
                                  h_hi[:, c, :], h_lo[:, c, :], c == 0, c == CT - 1)
                mm.then_inc(s_u, 1)

            def down(f, e):
                pe.wait_ge(s_fa, 2 * SLOTS * f + 2 * e + 2)
                pe.wait_ge(s_fp, 2 * SLOTS * f + 2 * e + 2)
                for c in range(CT):
                    mm = split_mm(Y[c][:, :], wd_hi[:, e, c * P:(c + 1) * P], wd_lo[:, e, c * P:(c + 1) * P],
                                  in_hi[:, :], in_lo[:, :], e == 0, e == SLOTS - 1)
                mm.then_inc(s_dn, 1)

            def max_item(b, item):
                kind, k = item
                i = ring_at[item]
                banks = (S[0], S[1]) if i % 2 == 0 else (S[2], S[3])
                if i >= 2:
                    pe.wait_ge(s_rd, RING * b + i - 1)
                elif i == 0:
                    pe.wait_ge(s_stk, 16 * STACK_DMAS * (b + 1))
                    pe.wait_ge(s_vb, TT * (b + 1))
                    if later(b):
                        pe.wait_ge(s_ce, b)
                if kind == "pair":
                    for j in range(2):
                        h, q = divmod(2 * k + j, TT)
                        mm = pe.matmul(banks[j], qs[0:ROWS, h, q * P:(q + 1) * P], ks[0:ROWS, h, :],
                                       start=True, stop=True)
                    mm.then_inc(s_smx, 1)
                else:
                    pe.wait_ge(s_mm, 4 * b + 2 * k + 2)
                    for part in range(2):
                        mm = pe.transpose(banks[0].bitcast(BF16)[0:32, part * P:(part + 1) * P],
                                          m12[:, k, part, :], ident_b[:, :])
                    mm.then_inc(s_smx, 1)

            def scores(b, g, last):
                quad, kt = divmod(g, TT)
                if g == 0:
                    pe.wait_ge(s_mrow[0], 32 * b + 32)
                    pe.wait_ge(s_rd, RING * (b + 1))
                if quad == 2 and kt == 0:
                    pe.wait_ge(s_mrow[1], 32 * b + 32)
                for j in range(4):
                    s, h = 4 * g + j, 4 * quad + j
                    if s >= 3:
                        pe.wait_ge(s_ex, TILES * b + s - 2)
                    elif s < 2 and not last:
                        pe.wait_ge(s_he1, 2 * b + s + 3)
                    pe.matmul(S[s % 3], ks[0:ROWS + SHIFT_ROWS, h, kt * P:(kt + 1) * P],
                              qs[0:ROWS + SHIFT_ROWS, h, :], start=True, stop=True).then_inc(s_st, 1)

            def times_v(b, g):
                quad, kt = divmod(g, TT)
                pe.wait_ge(s_ex, TILES * b + 4 * g + 4)
                if kt == 0 and quad:
                    pe.wait_ge(s_nm, NORM_STEPS * Q4 * b + NORM_STEPS * (quad - 1) + 1)
                for j in range(4):
                    h = 4 * quad + j
                    mm = pe.matmul(O[32 * j:32 * j + 32, :], v_s[:, kt, h * VW:h * VW + 32], pt[:, g % 2, j, :],
                                   start=(kt == 0), stop=(kt == TT - 1))
                mm.then_inc(s_pv, 1)

            def h_transposes(src, banks, s_ht):
                for c in range(CT):
                    for t in range(TT):
                        mm = pe.transpose(banks[c][:, t * P:(t + 1) * P], src[:, t, c * P:(c + 1) * P], ident[:, :])
                    mm.then_inc(s_ht, 1)

            def qk(n, t):
                if t == 0:
                    pe.wait_ge(s_hs1, 4 * n + 4)
                else:
                    pe.wait_ge(s_rope, ROPE_STEPS * n + 6)
                for r in range(2):
                    col = (2 * t + r) * P
                    for c in range(CT):
                        mm = split_mm(S[r], wqkv_hi[:, c, col:col + P], wqkv_lo[:, c, col:col + P],
                                      h1_hi[:, c, :], h1_lo[:, c, :], c == 0, c == CT - 1)
                    mm.then_inc(s_qk, 1)

            def v_proj(n):
                pe.wait_ge(s_rope, ROPE_STEPS * n + 12)
                for t in range(TT):
                    o = S[t // 2][:, (t % 2) * C:(t % 2 + 1) * C]
                    tok = slice(t * P, (t + 1) * P)
                    for c in range(CT):
                        pe.matmul(o, h1_hi[:, c, tok], wqkv_hi[:, c, 2 * C:], start=(c == 0), stop=False)
                        pe.matmul(o, h1_lo[:, c, tok], wqkv_hi[:, c, 2 * C:], start=False, stop=False)
                        mm = pe.matmul(o, upper(h1_hi[:, c, tok]), wqkv_lo[:, c, 2 * C:],
                                       start=False, stop=(c == CT - 1))
                    if t % 2:
                        mm.then_inc(s_v, 1)

            def projection(b):
                pe.wait_ge(s_nm, NORM_STEPS * Q4 * (b + 1))
                for c in range(CT):
                    for quad in range(Q4):
                        mm = pe.matmul(S[2 + c], pw_s[:, quad, c * P:(c + 1) * P], on[:, quad, :],
                                       start=(quad == 0), stop=(quad == Q4 - 1))
                    mm.then_inc(s_pj, 1)

            def back_transposes(src, s_t):
                for t in range(TT):
                    for c in range(CT):
                        o = (t % 2) * C + c * P
                        mm = pe.transpose(S[2 + t // 2][:, o:o + P], src[:, c, t * P:(t + 1) * P], ident[:, :])
                    if t % 2:
                        mm.then_inc(s_t, 1)

            def logits(b):
                pe.wait_ge(s_he2, 2 * b + 2)
                for c in range(CT):
                    mm = pe.matmul(S[2][0:E, :], gk_s[:, c, :], hf[:, c, :], start=(c == 0), stop=(c == CT - 1))
                mm.then_inc(s_lg, 1)

            def logit_transposes(b):
                pe.wait_ge(s_la, 2 * b + 1)
                pe.nop(nofuse=True)
                for t in range(TT):
                    mm = pe.transpose(S[3][:, t * E:(t + 1) * E], nrm[0:E, t * P:(t + 1) * P], ident[0:E, 0:E])
                mm.then_inc(s_lg, 1)

            def combine_transposes(f):
                pe.wait_ge(s_rt, RT_STEPS * (f + 1))
                for t in range(TT):
                    mm = pe.transpose(S[0][0:E, t * P:(t + 1) * P], comb[:, t, :], ident[:, :])
                mm.then_inc(s_ct, 1)

            def iteration(b, first=False, last=False):
                f = b - 1
                for e in range(SLOTS):
                    items = ring_of.get(e, [])
                    gs = groups_of.get(e, [])
                    if not first:
                        gate(f, e)
                    for item in items[0:2]:
                        max_item(b, item)
                    for g in gs[0:1]:
                        scores(b, g, last)
                        if g:
                            times_v(b, g - 1)
                    if e == 14:
                        times_v(b, GRP - 1)
                        if not last:
                            qk(b + 1, 0)
                    if e == 15 and not last:
                        qk(b + 1, 1)
                    if e == 16 and not last:
                        v_proj(b + 1)
                    if not first:
                        up(f, e)
                        if e == 0:
                            pe.wait_ge(s_vb, TT * (b + 1))
                            combine_transposes(f)
                        if e == 17:
                            logits(b)
                        if e:
                            down(f, e - 1)
                    elif e == 17:
                        logits(b)
                    for item in items[2:]:
                        max_item(b, item)
                    for g in gs[1:]:
                        scores(b, g, last)
                        times_v(b, g - 1)
                    if e == rows_slot[1] and not last:
                        pe.wait_ge(s_ln1, LN_STEPS * (b + 2))
                        pe.wait_ge(s_rd, RING * b + RING - 1)
                        h_transposes(xa, S[0:2], s_ht1)
                    if e == 14:
                        projection(b)
                    if e == 15:
                        pe.wait_ge(s_ae, 2 * b + 2)
                        back_transposes(hf, s_at)
                    if e == 16:
                        pe.wait_ge(s_ln2, LN_STEPS * (b + 1))
                        h_transposes(hft, S[2:4], s_ht2)
                    if e == 17:
                        logit_transposes(b)
                if not first:
                    down(f, SLOTS - 1)
                    y_back(f, 2 * b + 2)

            def y_back(f, router_reads):
                pe.wait_ge(s_la, router_reads)
                pe.wait_ge(s_ye, 2 * f + 2)
                back_transposes(ff, s_yt)

            pe.wait_ge(s_wmod, 16)
            pe.wait_ge(s_pre, SILU_STEPS)
            for k in range(6 * CT):
                for c in range(CT):
                    mm = pe.matmul(S[2][:, k * NB:(k + 1) * NB], wmod_v[:, c, k * P:(k + 1) * P],
                                   c_silu[:, c * NB:(c + 1) * NB], start=(c == 0), stop=(c == CT - 1))
            mm.then_inc(s_modp, 1)
            pe.wait_ge(s_ln1, LN_STEPS)
            h_transposes(xa, S[0:2], s_ht1)
            pe.wait_ge(s_pre, PRE_STEPS)
            qk(0, 0)
            qk(0, 1)
            v_proj(0)
            iteration(0, first=True)
            with pe.Fori(1, NB - 1) as b:
                iteration(b)
            iteration(NB - 1, last=True)
            f = NB - 1
            for e in range(SLOTS):
                gate(f, e)
                up(f, e)
                if e == 0:
                    combine_transposes(f)
                else:
                    down(f, e - 1)
            down(f, SLOTS - 1)
            y_back(f, 2 * NB)

        @block.vector
        def _(dve):
            def gated(f, e):
                dve.wait_ge(s_fa, 2 * SLOTS * f + 2 * e + 1)
                dve.scalar_tensor_tensor(ff[:, e % 2, :], ff[:, e % 2, :], 1.0, G[:, :], ALU.add,
                                         ALU.mult).then_inc(s_fd, 1)

            def times_up(f, e):
                dve.wait_ge(s_u, SLOTS * f + e + 1)
                dve.wait_ge(s_fp, 2 * SLOTS * f + 2 * e + 1)
                dve.tensor_tensor(ff[:, e % 2, :], ff[:, e % 2, :], U[:, :], ALU.mult).then_inc(s_fd, 1)

            def max_item(b, item):
                kind, k = item
                i = ring_at[item]
                lo = 0 if i % 2 == 0 else 2
                dve.wait_ge(s_smx, RING * b + i + 1)
                if kind == "rows":
                    src = S[lo].bitcast(BF16)[0:32, 0:2 * P]
                    dve.tensor_copy(mT[:, k, :, :].rearrange("r a q -> r (a q)"), src).then_inc(s_rd, 1)
                    return
                dve.tensor_reduce(mx[:, 2 * k:2 * k + 2], S4[:, lo:lo + 2, :], AX.X, ALU.max,
                                  negate=True).then_inc(s_rd, 1)
                if k in (PAIRS // 2 - 1, PAIRS - 1):
                    half = k // (PAIRS // 2)
                    m = mx[:, 32 * half:32 * half + 32]
                    dve.wait_ge(s_rd, RING * b + i + 1)
                    dve.tensor_copy(m12[:, half, 0, :], m).then_inc(s_mm, 1)
                    dve.wait_ge(s_mm, 4 * b + 2 * half + 1)
                    dve.tensor_tensor(m12[:, half, 1, :], m, m12[:, half, 0, :], ALU.subtract).then_inc(s_mm, 1)

            def norm(b, quad):
                k = NORM_STEPS * Q4 * b + NORM_STEPS * quad
                dve.wait_ge(s_pv, GRP * b + 4 * quad + 4)
                if quad:
                    dve.wait_ge(s_nm, k)
                elif later(b):
                    dve.wait_ge(s_cdw, 16 * b)
                else:
                    dve.wait_ge(s_rope, ROPE_STEPS)
                dve.transpose(nrm[:, :], O).then_inc(s_nm, 1)
                by_token = nrm[:, :].rearrange("p (k d) -> p k d", d=32)
                dve.wait_ge(s_nm, k + 1)
                dve.reciprocal(rec[:, :], by_token[:, :, HD]).then_inc(s_nm, 1)
                dve.wait_ge(s_nm, k + 2)
                dve.tensor_tensor(by_token, by_token, rec[:, :].unsqueeze(2).broadcast_to([P, N // 32, 32]),
                                  ALU.mult).then_inc(s_nm, 1)
                dve.wait_ge(s_nm, k + 3)
                dve.transpose(on[:, quad, :], nrm[:, :]).then_inc(s_nm, 1)

            def ln_stats(n, st, mv, ve, s_ln):
                for t in range(TT):
                    dve.bn_stats(st[:, t, :], xa[:, t, :]).then_inc(s_ln, 1)
                for t in range(TT):
                    dve.wait_ge(s_ln, LN_STEPS * n + TT)
                    dve.nop(nofuse=True)
                    dve.bn_aggr(mv[:, t, :], st[:, t, :]).then_inc(s_ln, 1)
                dve.wait_ge(s_ln, LN_STEPS * n + 2 * TT)
                dve.tensor_scalar(ve[:, :], mv[:, :, 1], LN_EPS, None, ALU.add).then_inc(s_ln, 1)

            def ln_rows(n, dst, mv, r, s_ln, s_r):
                dve.wait_ge(s_r, n + 1)
                for t in range(TT):
                    dve.tensor_scalar(dst[:, t, :], xa[:, t, :], mv[:, t, 0:1], r[:, t:t + 1],
                                      ALU.subtract, ALU.mult).then_inc(s_ln, 1)

            def split_h(n, hi, lo, s_he, s_hs):
                for c in range(CT):
                    dve.wait_ge(s_he, 2 * n + c + 1)
                    dve.tensor_copy(hi[:, c, :], hf[:, c, :]).then_inc(s_hs, 1)
                for c in range(CT):
                    dve.wait_ge(s_hs, 4 * n + c + 1)
                    dve.tensor_tensor(lo[:, c, :], hf[:, c, :], hi[:, c, :].bitcast(F32),
                                      ALU.subtract).then_inc(s_hs, 1)

            def rope(n, t):
                b0, b1 = qkb_s[:, 2 * t:2 * t + 1], qkb_s[:, 2 * t + 1:2 * t + 2]
                k = 6 * t
                for r in range(2):
                    c0, c1, op = ((cos_s, sin_s, ALU.subtract), (sin_s, cos_s, ALU.add))[r]
                    dve.wait_ge(s_qk, 4 * n + 2 * t + 1)
                    if t:
                        dve.wait_ge(s_pp, PART_STEPS * n + 3 + r)
                    dve.scalar_tensor_tensor(rope_a[r], S[0], b0, c0[:, :], ALU.add,
                                             ALU.mult).then_inc(s_rope, 1)
                    dve.wait_ge(s_qk, 4 * n + 2 * t + 2)
                    if k:
                        dve.wait_ge(s_rope, ROPE_STEPS * n + k)
                    elif later(n):
                        dve.wait_ge(s_nm, NORM_STEPS * Q4 * n)
                    dve.scalar_tensor_tensor(rope_b, S[1], b1, c1[:, :], ALU.add,
                                             ALU.mult).then_inc(s_rope, 1)
                    dve.wait_ge(s_rope, ROPE_STEPS * n + k + 2)
                    dve.tensor_tensor(rope_a[r], rope_a[r], rope_b, op).then_inc(s_rope, 1)
                    k += 3

            def v_bias(n):
                for t in range(TT):
                    dve.wait_ge(s_v, 2 * n + t // 2 + 1)
                    dve.tensor_tensor(v_heads[t][:, :, 0:HD],
                                      S[t // 2][:, (t % 2) * C:(t % 2 + 1) * C].rearrange("p (h d) -> p h d", h=H),
                                      vb_s[:, :].rearrange("p (h d) -> p h d", h=H), ALU.add).then_inc(s_vb, 1)

            def add_y(f):
                x2f = x2[:, :, :].rearrange("p t c -> p (t c)")
                dve.wait_ge(s_x2, 16 * f + 16)
                for i in range(2):
                    dve.wait_ge(s_yt, 2 * f + i + 1)
                    dve.tensor_tensor(x2f[:, i * N:(i + 1) * N], S[2 + i], x2f[:, i * N:(i + 1) * N],
                                      ALU.add).then_inc(s_ya, 1)

            def residual(b):
                xaf = xa[:, :, :].rearrange("p t c -> p (t c)")
                dve.wait_ge(s_xres, 16 * b + 16)
                for i in range(2):
                    dve.wait_ge(s_at, 2 * b + i + 1)
                    dve.tensor_tensor(xaf[:, i * N:(i + 1) * N], S[2 + i], xaf[:, i * N:(i + 1) * N],
                                      ALU.add).then_inc(s_rs, 1)

            def router(b):
                done = 0

                def step(ins):
                    nonlocal done
                    ins.then_inc(s_rt, 1)
                    done += 1
                    dve.wait_ge(s_rt, RT_STEPS * b + done)
                    dve.nop(nofuse=True)

                dve.wait_ge(s_la, 2 * b + 2)
                step(dve.tensor_scalar(rv[:, :, :], rv[:, :, :], 0.5, 0.5, ALU.mult, ALU.add))
                step(dve.tensor_tensor(rv[:, :, :], rv[:, :, :],
                                       gb_s[:, :].unsqueeze(1).broadcast_to([P, TT, E]), ALU.add))
                v4 = rv[:, :, :].rearrange("p t (g k) -> p (t g) k", k=4)
                p2, q2 = rp, rq
                step(dve.tensor_tensor(p2, v4[:, :, 0:2], v4[:, :, 2:4], ALU.max))
                step(dve.tensor_tensor(q2, v4[:, :, 0:2], v4[:, :, 2:4], ALU.min))
                top, mid, low, gs, rank = (rs_[:, i, :] for i in range(5))
                step(dve.tensor_tensor(top, p2[:, :, 0], p2[:, :, 1], ALU.max))
                step(dve.tensor_tensor(mid, p2[:, :, 0], p2[:, :, 1], ALU.min))
                step(dve.tensor_tensor(low, q2[:, :, 0], q2[:, :, 1], ALU.max))
                step(dve.tensor_tensor(mid, mid, low, ALU.max))
                step(dve.tensor_tensor(gs, top, mid, ALU.add))
                gs3 = gs.rearrange("p (t g) -> p t g", g=4)
                other = gs3.unsqueeze(2).broadcast_to([P, TT, 4, 4])
                own = gs3.unsqueeze(3).broadcast_to([P, TT, 4, 4])
                gt = rk[:, 0, :].rearrange("p (t a b) -> p t a b", a=4, b=4)
                eq = rk[:, 1, :].rearrange("p (t a b) -> p t a b", a=4, b=4)
                step(dve.tensor_tensor(gt, other, own, ALU.is_gt))
                step(dve.tensor_tensor(eq, other, own, ALU.is_equal))
                eq2 = rk[:, 1, :].rearrange("p (t a) -> p t a", t=TT)
                step(dve.tensor_tensor(eq2, eq2, tri[:, :].unsqueeze(1).broadcast_to([P, TT, 16]), ALU.mult))
                step(dve.tensor_tensor(rk[:, 0, :], rk[:, 0, :], rk[:, 1, :], ALU.add))
                step(dve.tensor_reduce(rank, rk[:, 0, :].rearrange("p (a b) -> p a b", b=4), AX.X, ALU.add))
                step(dve.tensor_scalar(rank, rank, 1.5, None, ALU.is_lt))
                step(dve.tensor_tensor(rw[:, :, 0:E].rearrange("p t (g k) -> p t g k", k=4),
                                       rv[:, :, :].rearrange("p t (g k) -> p t g k", k=4),
                                       rank.rearrange("p (t g) -> p t g", g=4).unsqueeze(3)
                                       .broadcast_to([P, TT, 4, 4]), ALU.mult))
                step(dve.memset(rw[:, :, E:E + 4], SENTINEL))
                for t in range(TT):
                    step(dve.max(r8[:, t, :], rw[:, t, 0:E]))
                step(dve.memset(r8[:, :, 4:8], SENTINEL))
                for t in range(TT):
                    step(dve.match_replace(rr[:, t, :], r8[:, t, :], rw[:, t, :], -SENTINEL))
                step(dve.tensor_tensor(rsel[:, :, :], rr[:, :, 0:E], rw[:, :, 0:E], ALU.not_equal))
                step(dve.tensor_tensor(rsel[:, :, :], rsel[:, :, :], rw[:, :, 0:E], ALU.mult))
                step(dve.tensor_reduce(rsum[:, 0, :], rsel[:, :, :], AX.X, ALU.add))
                step(dve.tensor_scalar(rsum[:, 1, :], rsum[:, 0, :], TOPK_EPS, None, ALU.add))
                step(dve.reciprocal(rsum[:, 2, :], rsum[:, 1, :]))
                step(dve.scalar_tensor_tensor(comb[:, :, :], rsel[:, :, :], 0.5 * ROUTE_SCALE,
                                              rsum[:, 2, :].unsqueeze(2).broadcast_to([P, TT, E]),
                                              ALU.mult, ALU.mult))
                assert done == RT_STEPS, done

            def iteration(b, first=False, last=False):
                f = b - 1
                for e in range(SLOTS):
                    items = ring_of.get(e, [])
                    gs = groups_of.get(e, [])
                    early = [g // 4 - 1 for g in gs[0:1] if g and g % 4 == 0]
                    late = [g // 4 - 1 for g in gs[1:] if g % 4 == 0]
                    if not first:
                        gated(f, e)
                    for item in items[0:2]:
                        max_item(b, item)
                    if e == 9 and not last:
                        split_h(b + 1, h1_hi, h1_lo, s_he1, s_hs1)
                    for quad in early:
                        norm(b, quad)
                    if e == 14:
                        norm(b, Q4 - 1)
                        if not last:
                            rope(b + 1, 0)
                    if e == 16:
                        ln_rows(b, hft, mv2, rstd2, s_ln2, s_rstd2)
                        if not last:
                            v_bias(b + 1)
                    if not first:
                        times_up(f, e)
                    for item in items[2:]:
                        max_item(b, item)
                    for quad in late:
                        norm(b, quad)
                    if not last:
                        if e == 6:
                            dve.wait_ge(s_xln, 16 * b + 32)
                            ln_stats(b + 1, st1, mv1, ve1, s_ln1)
                        if e == 7:
                            ln_rows(b + 1, xa, mv1, rstd1, s_ln1, s_rstd1)
                    if e == 15:
                        if not last:
                            rope(b + 1, 1)
                        residual(b)
                        dve.wait_ge(s_rs, 2 * b + 2)
                        ln_stats(b, st2, mv2, ve2, s_ln2)
                if first:
                    dve.wait_ge(s_wlo, 2 * SLOTS)
                split_h(b, h_hi, h_lo, s_he2, s_hs2)
                router(b)
                if not first:
                    add_y(f)

            pre = [0]

            def step(ins):
                ins.then_inc(s_pre, 1)
                pre[0] += 1
                dve.wait_ge(s_pre, pre[0])

            step(dve.memset(mhalf[:, :], -0.5))
            step(dve.memset(ks[ROWS:ROWS + SHIFT_ROWS, :, :], 1.0))
            step(dve.memset(v_s[:, :, 0:H * VW], 1.0))
            step(dve.memset(v_s[:, :, H * VW:], 0.0))
            dve.wait_ge(s_const, 16 * CONST_DMAS)
            step(dve.tensor_copy(ident_b[:, :], ident[:, :]))
            dve.wait_ge(s_cact, 1)
            step(dve.tensor_scalar(c_tanh, c_tanh, 0.5, 0.5, ALU.mult, ALU.add))
            step(dve.tensor_tensor(c_silu, c_tanh, c_raw, ALU.mult))
            assert pre[0] == SILU_STEPS
            dve.wait_ge(s_xln, 16)
            ln_stats(0, st1, mv1, ve1, s_ln1)
            ln_rows(0, xa, mv1, rstd1, s_ln1, s_rstd1)
            dve.wait_ge(s_wq, 16)
            step(dve.tensor_copy(wqkv_hi[:, :, :], wqkv_v))
            step(dve.tensor_tensor(wqkv_lo[:, :, :], wqkv_v, wqkv_hi[:, :, :].bitcast(F32), ALU.subtract))
            dve.wait_ge(s_modp, 1)
            mp = S[2][:, 0:6 * CT * NB].rearrange("p (k b) -> p b k", b=NB)
            tab = modB[:, :].rearrange("p (b k) -> p b k", k=MODS)
            for chunk, (dst, plus) in enumerate(((SA, 0.0), (CA, 1.0), (GA, 0.0), (SB, 0.0), (CB, 1.0), (GB, 0.0))):
                step(dve.tensor_scalar(tab[:, :, dst:dst + 2], mp[:, :, 2 * chunk:2 * chunk + 2], plus, None,
                                       ALU.add))
            for dst in (GA, GB):
                g = tab[:, :, dst:dst + 2]
                mag, sgn = (v.rearrange("p (b k) -> p b k", k=2) for v in (gate_mag, gate_sgn))
                step(dve.scalar_tensor_tensor(mag, g, -1.0, g, ALU.mult, ALU.max))
                step(dve.tensor_scalar(mag, mag, GATE_MIN, None, ALU.max))
                step(dve.tensor_scalar(sgn, g, 0.0, 2.0, ALU.is_ge, ALU.mult))
                step(dve.tensor_scalar(sgn, sgn, 1.0, None, ALU.subtract))
                step(dve.tensor_tensor(g, mag, sgn, ALU.mult))
            step(dve.tensor_tensor(tab[:, :, GPB:GPB + 2], tab[:, :, GA:GA + 2],
                                   pb_s[:, :].unsqueeze(1).broadcast_to([P, NB, 2]), ALU.mult))
            assert pre[0] == PRE_STEPS, pre[0]
            split_h(0, h1_hi, h1_lo, s_he1, s_hs1)
            rope(0, 0)
            rope(0, 1)
            v_bias(0)
            iteration(0, first=True)
            with dve.Fori(1, NB - 1) as b:
                iteration(b)
            iteration(NB - 1, last=True)
            for e in range(SLOTS):
                gated(NB - 1, e)
                times_up(NB - 1, e)
            add_y(NB - 1)


SILU_STEPS = 7
PRE_STEPS = SILU_STEPS + 2 + 6 + 10 + 1


def layouts(a):
    f32 = np.float32
    qkv = a["L0_attn_qkv_w"]
    wqk = qkv[:2 * C].reshape(2, H, HALF, 2, C).transpose(4, 0, 3, 2, 1).reshape(C, 2 * C)
    wqkv = np.concatenate([wqk, qkv[2 * C:].T], axis=1)
    qkb = a["L0_attn_qkv_b"][:2 * C].reshape(2, H, HALF, 2).transpose(2, 1, 0, 3).reshape(P, 4)
    pw = np.zeros((4, 32, Q4, C), f32)
    pw[:, :HD] = a["L0_attn_proj_w"].T.reshape(Q4, 4, HD, C).transpose(1, 2, 0, 3)
    def cols(w):
        return w.reshape(C, 2, M).transpose(1, 0, 2)
    gate = np.concatenate([cols(a["L0_ffn_sw_gate"]), a["L0_ffn_w_gate"]])
    up = np.concatenate([cols(a["L0_ffn_sw_up"]), a["L0_ffn_w_up"]])
    gu = np.stack([gate, up], 1).reshape(SLOTS, 2, CT, P, M).transpose(0, 3, 1, 2, 4).reshape(SLOTS, P, 4 * M)
    down = np.concatenate([a["L0_ffn_sw_down"].reshape(2, M, C), a["L0_ffn_w_down"]])
    inv = f32(1.0) / f32(10000.0) ** (np.arange(0, HD, 2, dtype=f32) / f32(HD))
    freqs = np.arange(N, dtype=f32)[None, :] * np.repeat(inv, H)[:, None]
    tri = (np.arange(4)[None, :] < np.arange(4)[:, None]).astype(f32).reshape(16)
    return {
        "x": a["L0_attn_x"], "cT": a["L0_c"].T, "wmod": a["L0_wmod"], "wqkv": wqkv, "qkb": qkb,
        "vb": a["L0_attn_qkv_b"][2 * C:], "pw": pw.reshape(P, Q4, C),
        "pb": a["L0_attn_proj_b"].reshape(CT, P).T, "gk": a["L0_ffn_gate_kernel"],
        "gb": a["L0_ffn_gate_bias"], "wffn": np.concatenate([gu, down], axis=2),
        "cosT": np.cos(freqs), "sinT": np.sin(freqs), "ident_in": np.eye(P, dtype=f32), "tri_in": tri,
    }


def kernel(**inputs):
    import concourse.bacc as bacc
    from concourse.bass_utils import run_bass_kernel_spmd

    nc = bacc.Bacc("TRN2", target_bir_lowering=False, num_devices=1)
    arrays = {k: np.ascontiguousarray(v) for k, v in layouts({k: np.asarray(v) for k, v in inputs.items()}).items()}
    args = {k: nc.dram_tensor(k, v.shape, F32, kind="ExternalInput").ap() for k, v in arrays.items()}
    out = nc.dram_tensor("out", (NB, N, C), F32, kind="ExternalOutput").ap()
    build(nc, **args, out=out)
    r = run_bass_kernel_spmd(nc, [arrays], core_ids=[0])
    return r.results[0]["out"]
```

```python
from contextlib import ExitStack

import numpy as np

import concourse.bass as bass
from concourse import mybir

F32 = mybir.dt.float32
F32R = mybir.dt.float32r
BF16 = mybir.dt.bfloat16
ALU = mybir.AluOpType
ACT = mybir.ActivationFunctionType
AX = mybir.AxisListType

P = 128
NB, N, C = 16, 512, 256
H, HD = 16, 16
HALF = HD // 2
E, M = 16, 128
SLOTS = E + 2
TT = N // P
CT = C // P
Q4 = H // 4
LN_EPS = 1e-5
TOPK_EPS = 1e-20
ROUTE_SCALE = 2.5
GATE_MIN = 0.25
SM_SCALE = float(HD) ** -0.5
CONST_DMAS = 10
SENTINEL = -3.0e38

Q_PART = (0, 0, 1, 1, 0, 2)
K_PART = (0, 1, 0, 1, 2, 0)
GROUPS = len(Q_PART)
ROWS = GROUPS * HD
SHIFT_ROWS = 2

SA, CA, GA, GPB, SB, CB, GB = range(0, 14, 2)
MODS = 14

PAIRS = H * TT // 2
RING = PAIRS + 2
TILES = H * TT
GRP = TILES // 4
LN_STEPS = 3 * TT + 1
ROPE_STEPS = 12
PART_STEPS = 8
NORM_AT = (0, 3, 7, 10)
NORM_STEPS = 14
RT_STEPS = 32
STACK_DMAS = 2 * 2 * GROUPS
SHARED = SLOTS - E
MAX_SLOTS = range(1, 8)
EXP_GROUPS = {8: 4, 9: 3, 10: 3, 11: 3, 12: 3}
FOLDED = 4
FOLD_SLOTS = MAX_SLOTS[:-1]
ROWS_SLOT = MAX_SLOTS[-1] + 1
FOLD_STEPS = 5
LOAD_X = 3
LN1_STATS, LN1_ROWS, LN1_TURN, LN1_SPLIT = 9, 10, 11, 12
TAIL = 13
assert TAIL + 4 == SLOTS - 1
VW = HD + 1


def build(nc, x, cT, wmod, wqkv, qkb, vb, pw, pb, gk, gb, wffn, cosT, sinT, ident_in, tri_in, out):
    ctx = ExitStack()
    with ctx:
        def sb(name, shape, dt=F32):
            return ctx.enter_context(nc.sbuf_tensor(name, shape, dt))

        def sem(name):
            return ctx.enter_context(nc.semaphore(name))

        wgu_hi = sb("wgu_hi", [P, SLOTS, 2, CT, M], F32R)
        wgu_lo = sb("wgu_lo", [P, SLOTS, 2, CT, M], BF16)
        wd_hi = sb("wd_hi", [P, SLOTS, C], F32R)
        wd_lo = sb("wd_lo", [P, SLOTS, C], BF16)
        wqkv_hi = sb("wqkv_hi", [P, CT, 3 * C], F32R)
        wqkv_lo = sb("wqkv_lo", [P, CT, 3 * C], BF16)
        pw_s = sb("pw_s", [P, CT, C])
        cos_s = sb("cos_s", [P, N])
        sin_s = sb("sin_s", [P, N])
        ident = sb("ident", [P, P])
        ident_b = sb("ident_b", [P, P], BF16)
        gk_s = sb("gk_s", [P, CT, E])
        gb_s = sb("gb_s", [P, E])
        vb_s = sb("vb_s", [P, C])
        qkb_s = sb("qkb_s", [P, 4])
        pb_s = sb("pb_s", [P, CT])
        tri = sb("tri", [P, 16])
        mhalf = sb("mhalf", [P, TT])
        modB = sb("modB", [P, NB * MODS])

        qs = sb("qs", [P, H, N], BF16)
        ks = sb("ks", [P, H, N], BF16)
        pt = sb("pt", [P, 2, 4, N])
        v_s = sb("v_s", [P, TT, H * VW + 32 - VW + 1])
        h1_hi = sb("h1_hi", [P, CT, N], F32R)
        h1_lo = sb("h1_lo", [P, CT, N], F32R)
        on = sb("on", [P, CT, N])
        both = sb("both", [P, N])
        nrm = sb("nrm", [P, N])
        rec = sb("rec", [P, N // 32])
        xa = sb("xa", [P, TT, C])
        x2 = sb("x2", [P, TT, C])
        hf = sb("hf", [P, CT, N])
        h_hi = sb("h_hi", [P, CT, N], F32R)
        h_lo = sb("h_lo", [P, CT, N], F32R)
        cb = sb("cb", [P, 3, N])
        ff = sb("ff", [P, 2, N])
        in_hi = sb("in_hi", [P, 2, N], F32R)
        in_lo = sb("in_lo", [P, 2, N], F32R)
        mx = sb("mx", [P, TILES])
        m12 = sb("m12", [P, 2, 2, 32], BF16)
        mT = sb("mT", [32, 2, 2, P], BF16)
        st1, st2 = sb("st1", [P, TT, 6]), sb("st2", [P, TT, 6])
        mv1, mv2 = sb("mv1", [P, TT, 2]), sb("mv2", [P, TT, 2])
        ve1, ve2 = sb("ve1", [P, TT]), sb("ve2", [P, TT])
        rstd1, rstd2 = sb("rstd1", [P, TT]), sb("rstd2", [P, TT])
        rv = sb("rv", [P, TT, E])

        cd = nc.dram_tensor("combine_rows", [E, N], F32, kind="Internal").ap()

        S4 = ctx.enter_context(nc.psum_tensor("S4", [P, 4, N], F32))
        S = [S4[:, i, :] for i in range(4)]
        G = ctx.enter_context(nc.psum_tensor("G", [P, N], F32))
        U = ctx.enter_context(nc.psum_tensor("U", [P, N], F32))
        Y = [ctx.enter_context(nc.psum_tensor(f"Y{i}", [P, N], F32)) for i in range(2)]
        O = S[3]

        wmod_v = qs[:, :, :].rearrange("p h n -> p (h n)").bitcast(F32)[:, 0:CT * 6 * C] \
            .rearrange("p (c n) -> p c n", c=CT)
        ptf = pt[:, :, :, :].rearrange("p a b n -> p (a b) n")
        wqkv_v = pt[:, :, :, :].rearrange("p a b n -> p (a b n)")[:, 0:CT * 3 * C] \
            .rearrange("p (c n) -> p c n", c=CT)
        parts = [ptf[:, 3 * t:3 * t + 3, :].rearrange("p a n -> p (a n)").bitcast(BF16)
                 .rearrange("p (j r n) -> p j r n", j=3, r=2) for t in range(2)]
        tiles_b = [ptf[:, i:i + FOLDED, :].rearrange("p a n -> p (a n)").bitcast(BF16)
                   .rearrange("p (j n) -> p j n", n=N) for i in (0, 8 - FOLDED)]
        rope_a, rope_b = (ptf[:, 6, :], ptf[:, 7, :]), nrm[:, :]
        v_heads = [v_s[:, t, 0:H * VW].rearrange("p (h d) -> p h d", h=H) for t in range(TT)]
        scratch = on[:, :, :].rearrange("p q n -> p (q n)")
        at = [0]

        def cut(*shape):
            n = int(np.prod(shape))
            v = scratch[:, at[0]:at[0] + n]
            at[0] += n
            names = "abc"[:len(shape)]
            return v.rearrange(f"p ({' '.join(names)}) -> p {' '.join(names)}",
                               **dict(zip(names[1:], shape[1:]))) if len(shape) > 1 else v

        rp, rq = cut(4 * TT, 2), cut(4 * TT, 2)
        rs_ = cut(5, 4 * TT)
        rk = cut(2, 16 * TT)
        rw, rr = cut(TT, E + 4), cut(TT, E + 4)
        r8 = cut(TT, 8)
        rsel = cut(TT, E)
        rsum = cut(3, TT)
        comb = cut(TT, E)
        c_raw = hf[:, 0, 0:CT * NB]
        c_tanh, c_silu = nrm[:, 0:CT * NB], nrm[:, CT * NB:2 * CT * NB]
        gate_mag, gate_sgn = nrm[:, 2 * CT * NB:2 * CT * NB + 2 * NB], nrm[:, 2 * CT * NB + 2 * NB:2 * CT * NB + 4 * NB]
        hft = hf[:, :, :].rearrange("p c n -> p (c n)").rearrange("p (t c) -> p t c", t=TT)
        stage = [x2[:, :, :].rearrange("p t c -> p (t c)"), ff[:, :, :].rearrange("p a n -> p (a n)")]

        def upper(ap):
            return ap.bitcast(BF16)[:, 1::2]

        s_const = sem("s_const")
        s_c, s_wmod, s_wq = sem("s_c"), sem("s_wmod"), sem("s_wq")
        s_pre = sem("s_pre")
        s_cact = sem("s_cact")
        s_modp = sem("s_modp")
        s_stage = [sem("s_stage0"), sem("s_stage1")]
        s_whi = sem("s_whi")
        s_wlo = sem("s_wlo")
        s_xln = sem("s_xln")
        s_xres = sem("s_xres")
        s_ln1, s_ln2 = sem("s_ln1"), sem("s_ln2")
        s_rstd1, s_rstd2 = sem("s_rstd1"), sem("s_rstd2")
        s_ht1, s_ht2 = sem("s_ht1"), sem("s_ht2")
        s_he1, s_he2 = sem("s_he1"), sem("s_he2")
        s_hs1 = sem("s_hs1")
        s_hh2 = sem("s_hh2")
        s_hs2 = sem("s_hs2")
        s_qk = sem("s_qk")
        s_v = sem("s_v")
        s_vb = sem("s_vb")
        s_rope = sem("s_rope")
        s_pa = sem("s_pa")
        s_pp = sem("s_pp")
        s_stk = sem("s_stk")
        s_smx = sem("s_smx")
        s_ra = sem("s_ra")
        s_rd = sem("s_rd")
        s_fo = sem("s_fo")
        s_mm = sem("s_mm")
        s_mrow = [sem("s_mrow0"), sem("s_mrow1")]
        s_st = sem("s_st")
        s_ex = sem("s_ex")
        s_pv = sem("s_pv")
        s_nm = sem("s_nm")
        s_pj = sem("s_pj")
        s_ae = sem("s_ae")
        s_at = sem("s_at")
        s_rs = sem("s_rs")
        s_lg = sem("s_lg")
        s_la = sem("s_la")
        s_rt = sem("s_rt")
        s_ct = sem("s_ct")
        s_ce = sem("s_ce")
        s_cdw = sem("s_cdw")
        s_cb = [sem(f"s_cb{i}") for i in range(3)]
        cb_uses = [len(range(i, E, 3)) for i in range(3)]
        s_g, s_u = sem("s_g"), sem("s_u")
        s_th = sem("s_th")
        s_ih = sem("s_ih")
        s_fd = sem("s_fd")
        s_fp = sem("s_fp")
        s_dn = sem("s_dn")
        s_ye = sem("s_ye")
        s_yt = sem("s_yt")
        s_ya = sem("s_ya")
        s_out = sem("s_out")
        s_x2 = sem("s_x2")

        def later(b):
            return not isinstance(b, int) or b > 0

        x_t = x.rearrange("b (t p) c -> b p t c", p=P)
        out_t = out.rearrange("b (t p) c -> b p t c", p=P)

        ring_of, folded = {}, {}
        start = 0
        for e in MAX_SLOTS:
            rows = 0 if e == MAX_SLOTS[4] else None
            if e in FOLD_SLOTS:
                own = ("pair", start) if rows is None else ("rows", rows)
                start += rows is None
                folded[e] = [("pair", start + j) for j in range(FOLDED)]
                start += FOLDED
                ring_of[e] = [folded[e][0], own] + folded[e][1:]
            else:
                ring_of[e] = [("pair", k) for k in range(start, PAIRS)]
        ring_of[ROWS_SLOT] = [("rows", 1)]
        ring = [item for items in ring_of.values() for item in items]
        ring_at = {item: i for i, item in enumerate(ring)}
        assert len(ring) == RING and len(ring_at) == RING
        by_act = [any(item in pairs for pairs in folded.values()) for item in ring]
        nth = [by_act[:i + 1].count(by_act[i]) for i in range(RING)]
        rows_bank = [S[1] if ring_at[("rows", 0)] % 2 else S[3], S[3]]
        ring_act, ring_dve = by_act.count(True), by_act.count(False)
        steps_of_folds = FOLD_STEPS * len(FOLD_SLOTS)

        def maxima_of(e):
            own = [item for item in ring_of[e] if item not in folded.get(e, [])]
            return own + [("fold", e - 1)] * (e - 1 in folded)

        half_done = {}
        for e in MAX_SLOTS:
            for item in maxima_of(e):
                pairs = [k for _, k in folded[item[1]]] if item[0] == "fold" else [item[1]] * (item[0] == "pair")
                for k in pairs:
                    half_done[k // (PAIRS // 2)] = item
        groups_of = {}
        start = 0
        for e, groups in EXP_GROUPS.items():
            groups_of[e] = list(range(start, start + groups))
            start += groups
        assert start == GRP
        rows_slot = [next(e for e in ring_of if ("rows", k) in ring_of[e]) for k in range(2)]

        block = ctx.enter_context(nc.Block())

        @block.sync
        def _(sp):
            def load_cb(f, x):
                if x < 3:
                    last = max(k for k in range(E) if k % 3 == x)
                    if later(f):
                        sp.wait_ge(s_fp, 2 * SLOTS * (f - 1) + 2 * (SHARED + last) + 1)
                else:
                    sp.wait_ge(s_fp, 2 * SLOTS * f + 2 * (SHARED + x - 3) + 1)
                sp.dma_start(cb[:, x % 3, :], cd[x, :].partition_broadcast(P)).then_inc(s_cb[x % 3], 16)

            def shift_rows(b, half):
                sp.wait_ge(s_rd, ring_dve * b + nth[ring_at[("rows", half)]])
                for part in range(SHIFT_ROWS):
                    dst = qs[ROWS + part:ROWS + part + 1, half * 8:half * 8 + 8, :] \
                        .rearrange("o h n -> o (h n)").rearrange("o (r q) -> o r q", q=P)
                    sp.dma_start(dst, mT[:, half, part, :]).then_inc(s_mrow[half], 16)

            def stack(n, t):
                for r in range(2):
                    sp.wait_ge(s_pp, PART_STEPS * n + 4 * t + 3 + r)
                    for g in range(GROUPS):
                        row = g * HD + r * HALF
                        dst = (qs, ks)[t][row:row + HALF, :, :]
                        src = parts[t][:, (Q_PART, K_PART)[t][g], r, :]
                        sp.dma_start(dst, src).then_inc(s_stk, 16)

            def load_x_ln(b, first):
                if first:
                    sp.wait_ge(s_ht1, 2)
                else:
                    sp.wait_ge(s_x2, 16 * b)
                    sp.nop(nofuse=True)
                sp.dma_start(xa[:, :, :], x_t[b + 1]).then_inc(s_xln, 16)

            def load_x_res(b, last):
                if last:
                    sp.wait_ge(s_x2, 16 * b)
                    sp.nop(nofuse=True)
                else:
                    sp.wait_ge(s_ht1, 2 * b + 4)
                    sp.nop(nofuse=True)
                sp.dma_start(xa[:, :, :], x_t[b]).then_inc(s_xres, 16)

            def store(f):
                sp.wait_ge(s_ya, 2 * f + 4)
                sp.nop(nofuse=True)
                sp.dma_start(out_t[f], x2[:, :, :]).then_inc(s_out, 16)

            def keep_residual(b, first):
                if first:
                    sp.wait_ge(s_wlo, 2 * SLOTS)
                else:
                    sp.wait_ge(s_out, 16 * b)
                    sp.nop(nofuse=True)
                sp.wait_ge(s_rs, 2 * b + 2)
                sp.dma_start(x2[:, :, :], xa[:, :, :]).then_inc(s_x2, 16)

            def combine_rows(b):
                sp.wait_ge(s_ce, b + 1)
                sp.nop(nofuse=True)
                for i in range(3):
                    if later(b):
                        sp.wait_ge(s_cb[i], 16 * cb_uses[i] * b)
                        sp.nop(nofuse=True)
                sp.dma_start(cd, nrm[0:E, :]).then_inc(s_cdw, 16)
                sp.wait_ge(s_cdw, 16 * b + 16)
                sp.nop(nofuse=True)
                for x in range(3):
                    load_cb(b, x)

            def iteration(b, first=False, last=False):
                f = b - 1
                for e in range(0 if first else 1, SLOTS):
                    if e == rows_slot[0] + 1:
                        shift_rows(b, 0)
                    if e == rows_slot[1] + 1:
                        shift_rows(b, 1)
                    if first:
                        if e >= 2:
                            sp.wait_ge(s_wlo, 2 * (e - 1))
                        sp.dma_start(stage[e % 2][:, 0:768], wffn[e]).then_inc(s_stage[e % 2], 16)
                    elif 3 <= e + 1 < E:
                        load_cb(f, e + 1)
                    if e == LOAD_X and not last:
                        load_x_ln(b, first)
                    if e == LN1_TURN:
                        load_x_res(b, last)
                    if e == TAIL and not last:
                        stack(b + 1, 0)
                    if e == TAIL + 1 and not last:
                        stack(b + 1, 1)
                combine_rows(b)
                if not first:
                    store(f)
                keep_residual(b, first)

            sp.dma_start(c_raw.rearrange("p (c b) -> p c b", c=CT),
                         cT.rearrange("(c p) b -> p c b", p=P)).then_inc(s_c, 16)
            sp.dma_start(xa[:, :, :], x_t[0]).then_inc(s_xln, 16)
            sp.dma_start(wmod_v, wmod.rearrange("(c p) n -> p c n", p=P)).then_inc(s_wmod, 16)
            for dst, src in ((ident[:, :], ident_in), (cos_s[:, :], cosT), (sin_s[:, :], sinT),
                             (gk_s[:, :, :], gk.rearrange("(c p) e -> p c e", p=P)),
                             (gb_s[:, :], gb.partition_broadcast(P)),
                             (vb_s[:, :], vb.partition_broadcast(P)),
                             (tri[:, :], tri_in.partition_broadcast(P)),
                             (qkb_s[:, :], qkb), (pb_s[:, :], pb), (pw_s[:, :, :], pw)):
                sp.dma_start(dst, src).then_inc(s_const, 16)
            sp.dma_start(wqkv_v, wqkv.rearrange("(c p) n -> p c n", p=P)).then_inc(s_wq, 16)
            stack(0, 0)
            stack(0, 1)
            iteration(0, first=True)
            with sp.Fori(1, NB - 1) as b:
                iteration(b)
            iteration(NB - 1, last=True)
            for x in range(3, E):
                load_cb(NB - 1, x)
            store(NB - 1)
            sp.wait_ge(s_out, 16 * NB)

        @block.gpsimd
        def _(pool):
            def combine(f, e):
                pool.wait_ge(s_fd, 2 * SLOTS * f + 2 * e + 1)
                if e < SHARED:
                    pool.nop(nofuse=True)
                    pool.tensor_scalar(ff[:, e % 2, :], ff[:, e % 2, :], 0.5, None,
                                       ALU.mult).then_inc(s_fp, 1)
                else:
                    x = e - SHARED
                    pool.wait_ge(s_cb[x % 3], 16 * cb_uses[x % 3] * f + 16 * (x // 3 + 1))
                    pool.tensor_tensor(ff[:, e % 2, :], ff[:, e % 2, :], cb[:, x % 3, :],
                                       ALU.mult).then_inc(s_fp, 1)

            def in_low(f, e):
                pool.wait_ge(s_ih, SLOTS * f + e + 1)
                if e >= 2 or later(f):
                    pool.wait_ge(s_dn, SLOTS * f + e - 1)
                pool.tensor_tensor(in_lo[:, e % 2, :], ff[:, e % 2, :], in_hi[:, e % 2, :].bitcast(F32),
                                   ALU.subtract).then_inc(s_fp, 1)

            def remainders(n, t, which, members=range(2)):
                for r in members:
                    k = PART_STEPS * n + 4 * t + 2 * which + r
                    pool.wait_ge(s_pa, k + 1)
                    dst = rope_a[r] if which == 0 else parts[t][:, 2, r, :]
                    pool.tensor_tensor(dst, rope_a[r], parts[t][:, which, r, :], ALU.subtract).then_inc(s_pp, 1)

            def rstd(n, s_ln, ve, r, s_r):
                pool.wait_ge(s_ln, LN_STEPS * n + 2 * TT + 1)
                pool.tensor_tensor(r[:, :], ve[:, :], mhalf[:, :], ALU.pow).then_inc(s_r, 1)

            def weights_lo(e):
                pool.wait_ge(s_whi, 2 * e + 1)
                st = stage[e % 2]
                pool.tensor_tensor(wgu_lo[:, e, :, :, :].rearrange("p a c m -> p (a c m)"), st[:, 0:512],
                                   wgu_hi[:, e, :, :, :].rearrange("p a c m -> p (a c m)").bitcast(F32),
                                   ALU.subtract).then_inc(s_wlo, 1)
                pool.wait_ge(s_whi, 2 * e + 2)
                pool.tensor_tensor(wd_lo[:, e, :], st[:, 512:768],
                                   wd_hi[:, e, :].bitcast(F32), ALU.subtract).then_inc(s_wlo, 1)

            def iteration(b, first=False, last=False):
                f = b - 1
                for e in range(0 if first else 1, SLOTS):
                    if first:
                        weights_lo(e)
                    if not first:
                        combine(f, e)
                    if not last:
                        if e == LN1_ROWS:
                            rstd(b + 1, s_ln1, ve1, rstd1, s_rstd1)
                        if e == TAIL:
                            remainders(b + 1, 0, 0)
                        if e == TAIL + 1:
                            remainders(b + 1, 1, 0, (1,))
                            remainders(b + 1, 1, 1)
                    if not first:
                        in_low(f, e)
                    if not last:
                        if e == TAIL:
                            remainders(b + 1, 0, 1)
                            remainders(b + 1, 1, 0, (0,))
                    if e == TAIL + 1:
                        rstd(b, s_ln2, ve2, rstd2, s_rstd2)
                combine(b, 0)
                in_low(b, 0)

            pool.wait_ge(s_pre, 1)
            rstd(0, s_ln1, ve1, rstd1, s_rstd1)
            for t in range(2):
                remainders(0, t, 0)
                remainders(0, t, 1)
            iteration(0, first=True)
            with pool.Fori(1, NB - 1) as b:
                iteration(b)
            iteration(NB - 1, last=True)
            for e in range(1, SLOTS):
                combine(NB - 1, e)
                in_low(NB - 1, e)

        @block.scalar
        def _(act):
            def mod(b, k):
                return modB[:, bass.ds(b * MODS + k, 1)]

            def gate_tanh(f, e):
                act.wait_ge(s_g, SLOTS * f + e + 1)
                if e >= 2 or later(f):
                    act.wait_ge(s_fp, 2 * SLOTS * f + 2 * e - 2)
                act.activation(ff[:, e % 2, :], G[:, :], ACT.Tanh, scale=0.5).then_inc(s_th, 1)

            def in_high(f, e):
                act.wait_ge(s_fd, 2 * SLOTS * f + 2 * e + 2)
                if e >= 2 or later(f):
                    act.wait_ge(s_dn, SLOTS * f + e - 1)
                act.activation(in_hi[:, e % 2, :], ff[:, e % 2, :], ACT.Copy).then_inc(s_ih, 1)

            def copy_pair(b, e, j):
                slot = FOLD_SLOTS.index(e)
                i = ring_at[folded[e][j]]
                act.wait_ge(s_smx, RING * b + i + 1)
                if slot >= 2:
                    act.wait_ge(s_fo, steps_of_folds * b + FOLD_STEPS * (slot - 1))
                lo = 2 if i % 2 == 0 else 0
                act.activation(tiles_b[slot % 2][:, 2 * j:2 * j + 2, :], S4[:, lo:lo + 2, :],
                               ACT.Copy).then_inc(s_ra, 1)

            def exp_group(b, g):
                for j in range(4):
                    s = 4 * g + j
                    act.wait_ge(s_st, TILES * b + s + 1)
                    if j == 0 and g == 1:
                        act.wait_ge(s_fo, steps_of_folds * (b + 1))
                    if j == 0 and g >= 2:
                        act.wait_ge(s_pv, GRP * b + g - 1)
                    act.activation(pt[:, g % 2, j, :], S[s % 3], ACT.Exp, scale=SM_SCALE).then_inc(s_ex, 1)

            def h_evac(b):
                for c in range(CT):
                    act.wait_ge(s_ht2, 2 * b + 2)
                    act.activation(hf[:, c, :], S[2 + c], ACT.Identity, scale=mod(b, CB + c),
                                   bias=mod(b, SB + c)).then_inc(s_he2, 1)

            def part_copies(n, t, which, members=range(2)):
                for r in members:
                    if which == 0:
                        act.wait_ge(s_rope, ROPE_STEPS * n + 6 * t + 3 * (r + 1))
                    else:
                        act.wait_ge(s_pp, PART_STEPS * n + 4 * t + r + 1)
                    act.activation(parts[t][:, which, r, :], rope_a[r], ACT.Copy).then_inc(s_pa, 1)

            def proj_evac(b, c):
                act.wait_ge(s_pj, 2 * b + c + 1)
                act.activation(hf[:, c, :], S[2 + c], ACT.Identity, scale=mod(b, GA + c),
                               bias=mod(b, GPB + c)).then_inc(s_ae, 1)

            def logits_copy(b):
                act.wait_ge(s_lg, 2 * b + 1)
                act.copy(nrm[0:E, :], S[2][0:E, :]).then_inc(s_la, 1)

            def router_tanh(b):
                act.wait_ge(s_lg, 2 * b + 2)
                if later(b):
                    act.wait_ge(s_rt, RT_STEPS * b)
                act.activation(rv[:, :, :].rearrange("p t e -> p (t e)"), S[3][:, 0:TT * E], ACT.Tanh,
                               scale=0.5).then_inc(s_la, 1)

            def combine_copy(f):
                act.wait_ge(s_ct, f + 1)
                act.copy(nrm[0:E, :], S[2][0:E, :]).then_inc(s_ce, 1)

            def y_evac(f, splits):
                act.wait_ge(s_dn, SLOTS * (f + 1))
                for c in range(CT):
                    act.wait_ge(s_hs2, splits)
                    act.activation(hf[:, c, :], Y[c][:, :], ACT.Copy, scale=mod(f, GB + c)).then_inc(s_ye, 1)

            def h_high(b, first):
                act.wait_ge(s_he2, 2 * b + 2)
                if not first:
                    act.wait_ge(s_u, SLOTS * b)
                for c in range(CT):
                    act.activation(h_hi[:, c, :], hf[:, c, :], ACT.Copy).then_inc(s_hh2, 1)

            def weights_hi(e):
                act.wait_ge(s_stage[e % 2], 16 * (e // 2 + 1))
                st = stage[e % 2]
                act.activation(wgu_hi[:, e, :, :, :].rearrange("p a c m -> p (a c m)"), st[:, 0:512],
                               ACT.Copy).then_inc(s_whi, 1)
                act.activation(wd_hi[:, e, :], st[:, 512:768], ACT.Copy).then_inc(s_whi, 1)

            def iteration(b, first=False, last=False):
                f = b - 1
                for e in range(0 if first else 1, SLOTS):
                    gs = groups_of.get(e, [])
                    if e == LN1_TURN:
                        for g in gs[0:1]:
                            exp_group(b, g)
                    if first:
                        weights_hi(e)
                    else:
                        gate_tanh(f, e)
                    for j in range(FOLDED - 1 if e in folded else 0):
                        copy_pair(b, e, j)
                    for g in gs[1:3] if e == LN1_TURN else gs[0:3]:
                        exp_group(b, g)
                    if e == TAIL and not last:
                        part_copies(b + 1, 0, 0)
                    if e == TAIL + 1 and not last:
                        part_copies(b + 1, 1, 0, (1,))
                        part_copies(b + 1, 1, 1)
                    if e == SLOTS - 1:
                        h_high(b, first)
                    if e == TAIL + 3:
                        logits_copy(b)
                    if not first:
                        in_high(f, e)
                    if e in folded:
                        copy_pair(b, e, FOLDED - 1)
                    for g in gs[3:]:
                        exp_group(b, g)
                    if e == TAIL:
                        if not last:
                            part_copies(b + 1, 0, 1)
                        proj_evac(b, 0)
                        if not last:
                            part_copies(b + 1, 1, 0, (0,))
                        proj_evac(b, 1)
                    if e == TAIL + 2:
                        h_evac(b)
                    if e == TAIL + 3:
                        router_tanh(b)
                gate_tanh(b, 0)
                if not first:
                    y_evac(f, 2 * b + 2)
                combine_copy(b)
                in_high(b, 0)

            act.wait_ge(s_c, 16)
            act.activation(c_tanh, c_raw, ACT.Tanh, scale=0.5).then_inc(s_cact, 1)
            act.wait_ge(s_pre, PRE_STEPS)
            for t in range(2):
                part_copies(0, t, 0)
                part_copies(0, t, 1)
            iteration(0, first=True)
            with act.Fori(1, NB - 1) as b:
                iteration(b)
            iteration(NB - 1, last=True)
            for e in range(1, SLOTS):
                gate_tanh(NB - 1, e)
                in_high(NB - 1, e)
            y_evac(NB - 1, 2 * NB)

        @block.tensor
        def _(pe):
            def split_mm(out_ap, w_hi, w_lo, x_hi, x_lo, first, last):
                pe.matmul(out_ap, w_hi, x_hi, start=first, stop=False)
                pe.matmul(out_ap, w_hi, x_lo, start=False, stop=False)
                return pe.matmul(out_ap, w_lo, upper(x_hi), start=False, stop=last)

            def gate(f, e, turned=False):
                if e == 0:
                    pe.wait_ge(s_hs2, 2 * f + 2)
                if e or later(f):
                    pe.wait_ge(s_fd, 2 * SLOTS * f + 2 * e - 1)
                if e == LN1_TURN and turned:
                    pe.wait_ge(s_he1, 2 * f + 6)
                for c in range(CT):
                    mm = split_mm(G[:, :], wgu_hi[:, e, 0, c, :], wgu_lo[:, e, 0, c, :],
                                  h_hi[:, c, :], h_lo[:, c, :], c == 0, c == CT - 1)
                mm.then_inc(s_g, 1)

            def up(f, e):
                if e or later(f):
                    pe.wait_ge(s_fd, 2 * SLOTS * f + 2 * e)
                for c in range(CT):
                    mm = split_mm(U[:, :], wgu_hi[:, e, 1, c, :], wgu_lo[:, e, 1, c, :],
                                  h_hi[:, c, :], h_lo[:, c, :], c == 0, c == CT - 1)
                mm.then_inc(s_u, 1)

            def down(f, e, halves=range(CT)):
                for c in halves:
                    if c == 0:
                        pe.wait_ge(s_ih, SLOTS * f + e + 1)
                        pe.wait_ge(s_fp, 2 * SLOTS * f + 2 * e + 2)
                    mm = split_mm(Y[c][:, :], wd_hi[:, e, c * P:(c + 1) * P], wd_lo[:, e, c * P:(c + 1) * P],
                                  in_hi[:, e % 2, :], in_lo[:, e % 2, :], e == 0, e == SLOTS - 1)
                    if c == CT - 1:
                        mm.then_inc(s_dn, 1)

            def max_item(b, item):
                kind, k = item
                i = ring_at[item]
                banks = (S[2], S[3]) if i % 2 == 0 else (S[0], S[1])
                if i >= 2:
                    if by_act[i - 2]:
                        pe.wait_ge(s_ra, ring_act * b + nth[i - 2])
                    else:
                        pe.wait_ge(s_rd, ring_dve * b + nth[i - 2])
                elif i == 0:
                    pe.wait_ge(s_stk, 16 * STACK_DMAS * (b + 1))
                    if later(b):
                        pe.wait_ge(s_ce, b)
                else:
                    pe.wait_ge(s_vb, TT * (b + 1))
                    if later(b):
                        pe.wait_ge(s_ya, 2 * b)
                if kind == "pair":
                    for j in range(2):
                        h, q = divmod(2 * k + j, TT)
                        mm = pe.matmul(banks[j], qs[0:ROWS, h, q * P:(q + 1) * P], ks[0:ROWS, h, :],
                                       start=True, stop=True)
                    mm.then_inc(s_smx, 1)
                else:
                    pe.wait_ge(s_mm, 4 * b + 2 * k + 2)
                    for part in range(2):
                        mm = pe.transpose(rows_bank[k].bitcast(BF16)[0:32, part * P:(part + 1) * P],
                                          m12[:, k, part, :], ident_b[:, :])
                    mm.then_inc(s_smx, 1)

            def scores_times_v(b, g):
                quad, kt = divmod(g, TT)
                if g == 0:
                    pe.wait_ge(s_mrow[0], 32 * b + 32)
                    pe.wait_ge(s_rd, ring_dve * (b + 1) - 2)
                if quad == 2 and kt == 0:
                    pe.wait_ge(s_mrow[1], 32 * b + 32)
                for j in range(4):
                    s, h = 4 * g + j, 4 * quad + j
                    if s >= 3:
                        pe.wait_ge(s_ex, TILES * b + s - 2)
                    elif s == 2:
                        pe.wait_ge(s_rd, ring_dve * (b + 1) - 1)
                    pe.matmul(S[s % 3], ks[0:ROWS + SHIFT_ROWS, h, kt * P:(kt + 1) * P],
                              qs[0:ROWS + SHIFT_ROWS, h, :], start=True, stop=True).then_inc(s_st, 1)
                    if g and j % 2:
                        times_v(b, g - 1, range(j - 1, j + 1))

            def times_v(b, g, heads=range(4)):
                quad, kt = divmod(g, TT)
                if g == 0 and 0 in heads:
                    pe.wait_ge(s_rd, ring_dve * (b + 1))
                if kt == 0 and quad and 0 in heads:
                    pe.wait_ge(s_nm, NORM_STEPS * b + NORM_AT[quad - 1] + 1)
                for j in heads:
                    h = 4 * quad + j
                    pe.wait_ge(s_ex, TILES * b + 4 * g + j + 1)
                    mm = pe.matmul(O[32 * j:32 * j + 32, :], v_s[:, kt, h * VW:h * VW + 32], pt[:, g % 2, j, :],
                                   start=(kt == 0), stop=(kt == TT - 1))
                if 3 in heads:
                    mm.then_inc(s_pv, 1)

            def h_transposes(src, banks, s_ht):
                for c in range(CT):
                    for t in range(TT):
                        mm = pe.transpose(banks[c][:, t * P:(t + 1) * P], src[:, t, c * P:(c + 1) * P], ident[:, :])
                    mm.then_inc(s_ht, 1)

            def qk(n, t):
                if t == 0:
                    pe.wait_ge(s_hs1, 4 * n + 4)
                else:
                    pe.wait_ge(s_rope, ROPE_STEPS * n + 6)
                for r in range(2):
                    col = (2 * t + r) * P
                    for c in range(CT):
                        mm = split_mm(S[r], wqkv_hi[:, c, col:col + P], wqkv_lo[:, c, col:col + P],
                                      h1_hi[:, c, :], h1_lo[:, c, :], c == 0, c == CT - 1)
                    mm.then_inc(s_qk, 1)

            def v_proj(n):
                pe.wait_ge(s_rope, ROPE_STEPS * n + 12)
                for t in range(TT):
                    o = S[t // 2][:, (t % 2) * C:(t % 2 + 1) * C]
                    tok = slice(t * P, (t + 1) * P)
                    for c in range(CT):
                        pe.matmul(o, h1_hi[:, c, tok], wqkv_hi[:, c, 2 * C:], start=(c == 0), stop=False)
                        pe.matmul(o, h1_lo[:, c, tok], wqkv_hi[:, c, 2 * C:], start=False, stop=False)
                        mm = pe.matmul(o, upper(h1_hi[:, c, tok]), wqkv_lo[:, c, 2 * C:],
                                       start=False, stop=(c == CT - 1))
                    if t % 2:
                        mm.then_inc(s_v, 1)

            def projection(b, c):
                if c == 0:
                    pe.wait_ge(s_nm, NORM_STEPS * (b + 1))
                for i in range(CT):
                    mm = pe.matmul(S[2 + c], pw_s[:, i, c * P:(c + 1) * P], on[:, i, :],
                                   start=(i == 0), stop=(i == CT - 1))
                mm.then_inc(s_pj, 1)

            def back_transposes(src, banks, s_t):
                for t in range(TT):
                    for c in range(CT):
                        o = (t % 2) * C + c * P
                        mm = pe.transpose(banks[t // 2][:, o:o + P], src[:, c, t * P:(t + 1) * P], ident[:, :])
                    if t % 2:
                        mm.then_inc(s_t, 1)

            def logits(b):
                pe.wait_ge(s_he2, 2 * b + 2)
                for c in range(CT):
                    mm = pe.matmul(S[2][0:E, :], gk_s[:, c, :], hf[:, c, :], start=(c == 0), stop=(c == CT - 1))
                mm.then_inc(s_lg, 1)

            def logit_transposes(b):
                pe.wait_ge(s_la, 2 * b + 1)
                pe.nop(nofuse=True)
                for t in range(TT):
                    mm = pe.transpose(S[3][:, t * E:(t + 1) * E], nrm[0:E, t * P:(t + 1) * P], ident[0:E, 0:E])
                mm.then_inc(s_lg, 1)

            def combine_transposes(f):
                pe.wait_ge(s_rt, RT_STEPS * (f + 1))
                for t in range(TT):
                    mm = pe.transpose(S[2][0:E, t * P:(t + 1) * P], comb[:, t, :], ident[:, :])
                mm.then_inc(s_ct, 1)

            def iteration(b, first=False, last=False):
                f = b - 1
                for e in range(0 if first else 1, SLOTS):
                    items = ring_of.get(e, [])
                    gs = groups_of.get(e, [])
                    if e == LN1_TURN and not last:
                        pe.wait_ge(s_ln1, LN_STEPS * (b + 2))
                        if not first:
                            pe.wait_ge(s_fd, 2 * SLOTS * f + 2 * e)
                        h_transposes(xa, (G[:, :], U[:, :]), s_ht1)
                        for g in gs[0:1]:
                            scores_times_v(b, g)
                    if not first and e > 1:
                        gate(f, e, turned=not last)
                    if e != LN1_TURN or last:
                        for g in gs[0:1]:
                            scores_times_v(b, g)
                    if e in MAX_SLOTS:
                        for item in items[0:2]:
                            max_item(b, item)
                    if e == TAIL:
                        times_v(b, GRP - 1)
                        if not last:
                            qk(b + 1, 0)
                    if not first:
                        up(f, e)
                    if e == TAIL + 2 and not last:
                        v_proj(b + 1)
                    for item in items[2:3]:
                        max_item(b, item)
                    if e == ROWS_SLOT:
                        if not first:
                            down(f, e - 1, (0,))
                        max_item(b, ("rows", 1))
                    for g in gs[1:2]:
                        scores_times_v(b, g)
                    if not first and e != ROWS_SLOT:
                        down(f, e - 1, (0,))
                    if e == TAIL + 3:
                        logits(b)
                    for item in items[3:4]:
                        max_item(b, item)
                    for g in gs[2:3]:
                        scores_times_v(b, g)
                    if not first:
                        down(f, e - 1, (1,))
                    for item in items[4:]:
                        max_item(b, item)
                    for g in gs[3:]:
                        scores_times_v(b, g)
                    if e == TAIL:
                        projection(b, 0)
                        if not last:
                            qk(b + 1, 1)
                        projection(b, 1)
                    if e == TAIL + 1:
                        pe.wait_ge(s_ae, 2 * b + 2)
                        back_transposes(hf, S[2:4], s_at)
                    if e == TAIL + 2:
                        pe.wait_ge(s_ln2, LN_STEPS * (b + 1))
                        h_transposes(hft, S[2:4], s_ht2)
                    if e == TAIL + 3:
                        logit_transposes(b)
                gate(b, 0)
                up(b, 0)
                if not first:
                    down(f, SLOTS - 1)
                gate(b, 1)
                combine_transposes(b)
                if not first:
                    if not last:
                        pe.wait_ge(s_vb, TT * (b + 2))
                    y_back(f)

            def y_back(f):
                pe.wait_ge(s_ye, 2 * f + 2)
                back_transposes(hf, S[0:2], s_yt)

            pe.wait_ge(s_wmod, 16)
            pe.wait_ge(s_pre, SILU_STEPS)
            for k in range(6 * CT):
                for c in range(CT):
                    mm = pe.matmul(S[2][:, k * NB:(k + 1) * NB], wmod_v[:, c, k * P:(k + 1) * P],
                                   c_silu[:, c * NB:(c + 1) * NB], start=(c == 0), stop=(c == CT - 1))
            mm.then_inc(s_modp, 1)
            pe.wait_ge(s_ln1, LN_STEPS)
            h_transposes(xa, S[0:2], s_ht1)
            pe.wait_ge(s_pre, PRE_STEPS)
            qk(0, 0)
            qk(0, 1)
            v_proj(0)
            iteration(0, first=True)
            with pe.Fori(1, NB - 1) as b:
                iteration(b)
            iteration(NB - 1, last=True)
            f = NB - 1
            for e in range(1, SLOTS):
                if e > 1:
                    gate(f, e)
                up(f, e)
                down(f, e - 1)
            down(f, SLOTS - 1)
            y_back(f)

        @block.vector
        def _(dve):
            def mod(b, k):
                return modB[:, bass.ds(b * MODS + k, 1)]

            def gated(f, e):
                dve.wait_ge(s_th, SLOTS * f + e + 1)
                dve.scalar_tensor_tensor(ff[:, e % 2, :], ff[:, e % 2, :], 1.0, G[:, :], ALU.add,
                                         ALU.mult).then_inc(s_fd, 1)

            def times_up(f, e):
                dve.wait_ge(s_u, SLOTS * f + e + 1)
                dve.wait_ge(s_fp, 2 * SLOTS * f + 2 * e + 1)
                dve.tensor_tensor(ff[:, e % 2, :], ff[:, e % 2, :], U[:, :], ALU.mult).then_inc(s_fd, 1)

            def max_item(b, item):
                kind, k = item
                if kind == "fold":
                    return fold(b, k)
                i = ring_at[item]
                lo = 2 if i % 2 == 0 else 0
                dve.wait_ge(s_smx, RING * b + i + 1)
                if kind == "rows":
                    src = rows_bank[k].bitcast(BF16)[0:32, 0:2 * P]
                    dve.tensor_copy(mT[:, k, :, :].rearrange("r a q -> r (a q)"), src).then_inc(s_rd, 1)
                    return
                dve.tensor_reduce(mx[:, 2 * k:2 * k + 2], S4[:, lo:lo + 2, :], AX.X, ALU.max,
                                  negate=True).then_inc(s_rd, 1)
                for half in range(2):
                    if half_done[half] == item:
                        dve.wait_ge(s_rd, ring_dve * b + nth[i])
                        split_maxima(b, half)

            def fold(b, e):
                slot = FOLD_SLOTS.index(e)
                k = steps_of_folds * b + FOLD_STEPS * slot
                tiles = tiles_b[slot % 2]
                dve.wait_ge(s_ra, ring_act * b + FOLDED * (slot + 1))
                n = N
                for step in range(FOLD_STEPS - 1):
                    n //= 2
                    if step:
                        dve.wait_ge(s_fo, k + step)
                    dve.tensor_tensor(tiles[:, :, 0:n], tiles[:, :, 0:n], tiles[:, :, n:2 * n],
                                      ALU.max).then_inc(s_fo, 1)
                dve.wait_ge(s_fo, k + FOLD_STEPS - 1)
                first = folded[e][0][1]
                dve.tensor_reduce(mx[:, 2 * first:2 * (first + FOLDED)], tiles[:, :, 0:n], AX.X, ALU.max,
                                  negate=True).then_inc(s_fo, 1)
                for half in range(2):
                    if half_done[half] == ("fold", e):
                        dve.wait_ge(s_fo, k + FOLD_STEPS)
                        split_maxima(b, half)

            def split_maxima(b, half):
                m = mx[:, 32 * half:32 * half + 32]
                dve.tensor_copy(m12[:, half, 0, :], m).then_inc(s_mm, 1)
                dve.wait_ge(s_mm, 4 * b + 2 * half + 1)
                dve.tensor_tensor(m12[:, half, 1, :], m, m12[:, half, 0, :], ALU.subtract).then_inc(s_mm, 1)

            def norm(b, quad):
                k = NORM_STEPS * b + NORM_AT[quad]
                dve.wait_ge(s_pv, GRP * b + 4 * quad + 4)
                if quad:
                    dve.wait_ge(s_nm, k)
                elif later(b):
                    dve.wait_ge(s_cdw, 16 * b)
                else:
                    dve.wait_ge(s_rope, ROPE_STEPS)
                dve.transpose(nrm[:, :], O).then_inc(s_nm, 1)
                by_token = nrm[:, :].rearrange("p (k d) -> p k d", d=32)
                dve.wait_ge(s_nm, k + 1)
                dve.reciprocal(rec[:, :], by_token[:, :, HD]).then_inc(s_nm, 1)
                dve.wait_ge(s_nm, k + 2)
                side = quad % 2 * HD
                dve.tensor_tensor(both[:, :].rearrange("p (k d) -> p k d", d=32)[:, :, side:side + HD],
                                  by_token[:, :, 0:HD], rec[:, :].unsqueeze(2).broadcast_to([P, N // 32, HD]),
                                  ALU.mult).then_inc(s_nm, 1)
                if quad % 2:
                    dve.wait_ge(s_nm, k + 3)
                    dve.transpose(on[:, quad // 2, :], both[:, :]).then_inc(s_nm, 1)

            def ln_stats(n, st, mv, ve, s_ln):
                for t in range(TT):
                    dve.bn_stats(st[:, t, :], xa[:, t, :]).then_inc(s_ln, 1)
                for t in range(TT):
                    dve.wait_ge(s_ln, LN_STEPS * n + TT)
                    dve.nop(nofuse=True)
                    dve.bn_aggr(mv[:, t, :], st[:, t, :]).then_inc(s_ln, 1)
                dve.wait_ge(s_ln, LN_STEPS * n + 2 * TT)
                dve.tensor_scalar(ve[:, :], mv[:, :, 1], LN_EPS, None, ALU.add).then_inc(s_ln, 1)

            def ln_rows(n, dst, mv, r, s_ln, s_r):
                dve.wait_ge(s_r, n + 1)
                for t in range(TT):
                    dve.tensor_scalar(dst[:, t, :], xa[:, t, :], mv[:, t, 0:1], r[:, t:t + 1],
                                      ALU.subtract, ALU.mult).then_inc(s_ln, 1)

            def evacuate_h1(n, banks):
                for c in range(CT):
                    dve.wait_ge(s_ht1, 2 * n + c + 1)
                    dve.tensor_scalar(hf[:, c, :], banks[c], mod(n, CA + c), mod(n, SA + c),
                                      ALU.mult, ALU.add).then_inc(s_he1, 1)

            def split_h1(n):
                for c in range(CT):
                    dve.wait_ge(s_he1, 2 * n + c + 1)
                    dve.tensor_copy(h1_hi[:, c, :], hf[:, c, :]).then_inc(s_hs1, 1)
                for c in range(CT):
                    dve.wait_ge(s_hs1, 4 * n + c + 1)
                    dve.tensor_tensor(h1_lo[:, c, :], hf[:, c, :], h1_hi[:, c, :].bitcast(F32),
                                      ALU.subtract).then_inc(s_hs1, 1)

            def h_low(b):
                for c in range(CT):
                    dve.wait_ge(s_hh2, 2 * b + c + 1)
                    dve.tensor_tensor(h_lo[:, c, :], hf[:, c, :], h_hi[:, c, :].bitcast(F32),
                                      ALU.subtract).then_inc(s_hs2, 1)

            def rope(n, t):
                b0, b1 = qkb_s[:, 2 * t:2 * t + 1], qkb_s[:, 2 * t + 1:2 * t + 2]
                k = 6 * t
                for r in range(2):
                    c0, c1, op = ((cos_s, sin_s, ALU.subtract), (sin_s, cos_s, ALU.add))[r]
                    dve.wait_ge(s_qk, 4 * n + 2 * t + 1)
                    if t:
                        dve.wait_ge(s_pp, PART_STEPS * n + 3 + r)
                    dve.scalar_tensor_tensor(rope_a[r], S[0], b0, c0[:, :], ALU.add,
                                             ALU.mult).then_inc(s_rope, 1)
                    dve.wait_ge(s_qk, 4 * n + 2 * t + 2)
                    if k:
                        dve.wait_ge(s_rope, ROPE_STEPS * n + k)
                    elif later(n):
                        dve.wait_ge(s_nm, NORM_STEPS * n)
                    dve.scalar_tensor_tensor(rope_b, S[1], b1, c1[:, :], ALU.add,
                                             ALU.mult).then_inc(s_rope, 1)
                    dve.wait_ge(s_rope, ROPE_STEPS * n + k + 2)
                    dve.tensor_tensor(rope_a[r], rope_a[r], rope_b, op).then_inc(s_rope, 1)
                    k += 3

            def v_bias(n):
                for t in range(TT):
                    dve.wait_ge(s_v, 2 * n + t // 2 + 1)
                    dve.tensor_tensor(v_heads[t][:, :, 0:HD],
                                      S[t // 2][:, (t % 2) * C:(t % 2 + 1) * C].rearrange("p (h d) -> p h d", h=H),
                                      vb_s[:, :].rearrange("p (h d) -> p h d", h=H), ALU.add).then_inc(s_vb, 1)

            def add_y(f):
                x2f = x2[:, :, :].rearrange("p t c -> p (t c)")
                dve.wait_ge(s_x2, 16 * f + 16)
                for i in range(2):
                    dve.wait_ge(s_yt, 2 * f + i + 1)
                    dve.tensor_tensor(x2f[:, i * N:(i + 1) * N], S[i], x2f[:, i * N:(i + 1) * N],
                                      ALU.add).then_inc(s_ya, 1)

            def residual(b):
                xaf = xa[:, :, :].rearrange("p t c -> p (t c)")
                dve.wait_ge(s_xres, 16 * b + 16)
                for i in range(2):
                    dve.wait_ge(s_at, 2 * b + i + 1)
                    dve.tensor_tensor(xaf[:, i * N:(i + 1) * N], S[2 + i], xaf[:, i * N:(i + 1) * N],
                                      ALU.add).then_inc(s_rs, 1)

            top, mid, low, gs, rank = (rs_[:, i, :] for i in range(5))
            done = [0]

            def count(ins):
                ins.then_inc(s_rt, 1)
                done[0] += 1

            def router_step(b, ins):
                count(ins)
                dve.wait_ge(s_rt, RT_STEPS * b + done[0])

            def group_scores(b):
                done[0] = 0

                def step(ins):
                    router_step(b, ins)

                count(dve.memset(rw[:, :, E:E + 4], SENTINEL))
                dve.wait_ge(s_la, 2 * b + 2)
                step(dve.tensor_scalar(rv[:, :, :], rv[:, :, :], 0.5, 0.5, ALU.mult, ALU.add))
                step(dve.tensor_tensor(rv[:, :, :], rv[:, :, :],
                                       gb_s[:, :].unsqueeze(1).broadcast_to([P, TT, E]), ALU.add))
                v4 = rv[:, :, :].rearrange("p t (g k) -> p (t g) k", k=4)
                p2, q2 = rp, rq
                count(dve.tensor_tensor(p2, v4[:, :, 0:2], v4[:, :, 2:4], ALU.max))
                step(dve.tensor_tensor(q2, v4[:, :, 0:2], v4[:, :, 2:4], ALU.min))
                count(dve.tensor_tensor(top, p2[:, :, 0], p2[:, :, 1], ALU.max))
                count(dve.tensor_tensor(mid, p2[:, :, 0], p2[:, :, 1], ALU.min))
                step(dve.tensor_tensor(low, q2[:, :, 0], q2[:, :, 1], ALU.max))
                step(dve.tensor_tensor(mid, mid, low, ALU.max))
                step(dve.tensor_tensor(gs, top, mid, ALU.add))

            def group_ranks(b):
                def step(ins):
                    router_step(b, ins)

                dve.wait_ge(s_rt, RT_STEPS * b + done[0])
                gs3 = gs.rearrange("p (t g) -> p t g", g=4)
                other = gs3.unsqueeze(2).broadcast_to([P, TT, 4, 4])
                own = gs3.unsqueeze(3).broadcast_to([P, TT, 4, 4])
                gt = rk[:, 0, :].rearrange("p (t a b) -> p t a b", a=4, b=4)
                eq = rk[:, 1, :].rearrange("p (t a b) -> p t a b", a=4, b=4)
                count(dve.tensor_tensor(gt, other, own, ALU.is_gt))
                step(dve.tensor_tensor(eq, other, own, ALU.is_equal))
                eq2 = rk[:, 1, :].rearrange("p (t a) -> p t a", t=TT)
                step(dve.tensor_tensor(eq2, eq2, tri[:, :].unsqueeze(1).broadcast_to([P, TT, 16]), ALU.mult))
                step(dve.tensor_tensor(rk[:, 0, :], rk[:, 0, :], rk[:, 1, :], ALU.add))
                step(dve.tensor_reduce(rank, rk[:, 0, :].rearrange("p (a b) -> p a b", b=4), AX.X, ALU.add))
                step(dve.tensor_scalar(rank, rank, 1.5, None, ALU.is_lt))
                step(dve.tensor_tensor(rw[:, :, 0:E].rearrange("p t (g k) -> p t g k", k=4),
                                       rv[:, :, :].rearrange("p t (g k) -> p t g k", k=4),
                                       rank.rearrange("p (t g) -> p t g", g=4).unsqueeze(3)
                                       .broadcast_to([P, TT, 4, 4]), ALU.mult))

            def pick_experts(b):
                def step(ins):
                    router_step(b, ins)

                dve.wait_ge(s_rt, RT_STEPS * b + done[0])
                dve.nop(nofuse=True)
                for t in range(TT):
                    count(dve.max(r8[:, t, :], rw[:, t, 0:E]))
                dve.wait_ge(s_rt, RT_STEPS * b + done[0])
                step(dve.memset(r8[:, :, 4:8], SENTINEL))
                dve.nop(nofuse=True)
                for t in range(TT):
                    count(dve.match_replace(rr[:, t, :], r8[:, t, :], rw[:, t, :], -SENTINEL))
                dve.wait_ge(s_rt, RT_STEPS * b + done[0])
                step(dve.tensor_tensor(rsel[:, :, :], rr[:, :, 0:E], rw[:, :, 0:E], ALU.not_equal))
                step(dve.tensor_tensor(rsel[:, :, :], rsel[:, :, :], rw[:, :, 0:E], ALU.mult))
                step(dve.tensor_reduce(rsum[:, 0, :], rsel[:, :, :], AX.X, ALU.add))
                step(dve.tensor_scalar(rsum[:, 1, :], rsum[:, 0, :], TOPK_EPS, None, ALU.add))
                step(dve.reciprocal(rsum[:, 2, :], rsum[:, 1, :]))
                step(dve.scalar_tensor_tensor(comb[:, :, :], rsel[:, :, :], 0.5 * ROUTE_SCALE,
                                              rsum[:, 2, :].unsqueeze(2).broadcast_to([P, TT, E]),
                                              ALU.mult, ALU.mult))
                assert done[0] == RT_STEPS, done

            def iteration(b, first=False, last=False):
                f = b - 1
                for e in range(0 if first else 1, SLOTS):
                    items = ring_of.get(e, [])
                    gs = groups_of.get(e, [])
                    early = [g // 4 - 1 for g in gs[0:1] if g and g % 4 == 0]
                    late = [g // 4 - 1 for g in gs[1:] if g % 4 == 0]
                    if e == LN1_TURN and not last:
                        evacuate_h1(b + 1, (G[:, :], U[:, :]))
                    if not first:
                        gated(f, e)
                    work = maxima_of(e) if e in ring_of else []
                    for item in work[0:1]:
                        max_item(b, item)
                    if e == LN1_SPLIT and not last:
                        split_h1(b + 1)
                    for quad in early:
                        norm(b, quad)
                    if e == TAIL:
                        norm(b, Q4 - 1)
                        if not last:
                            rope(b + 1, 0)
                    if e == TAIL + 2:
                        ln_rows(b, hft, mv2, rstd2, s_ln2, s_rstd2)
                    if e == SLOTS - 1:
                        if first:
                            dve.wait_ge(s_wlo, 2 * SLOTS)
                        h_low(b)
                    if not first:
                        times_up(f, e)
                    if e == TAIL + 2 and not last:
                        v_bias(b + 1)
                    for item in work[1:]:
                        max_item(b, item)
                    for quad in late:
                        norm(b, quad)
                    if not last:
                        if e == LN1_STATS:
                            dve.wait_ge(s_xln, 16 * b + 32)
                            ln_stats(b + 1, st1, mv1, ve1, s_ln1)
                        if e == LN1_ROWS:
                            ln_rows(b + 1, xa, mv1, rstd1, s_ln1, s_rstd1)
                    if e == TAIL and not last:
                        rope(b + 1, 1)
                    if e == TAIL + 1:
                        residual(b)
                        dve.wait_ge(s_rs, 2 * b + 2)
                        ln_stats(b, st2, mv2, ve2, s_ln2)
                    if e == TAIL + 3:
                        group_scores(b)
                group_ranks(b)
                gated(b, 0)
                pick_experts(b)
                times_up(b, 0)
                if first:
                    dve.nop(nofuse=True).then_inc(s_ya, 2)
                else:
                    add_y(f)

            pre = [0]

            def step(ins):
                ins.then_inc(s_pre, 1)
                pre[0] += 1
                dve.wait_ge(s_pre, pre[0])

            step(dve.memset(mhalf[:, :], -0.5))
            step(dve.memset(ks[ROWS:ROWS + SHIFT_ROWS, :, :], 1.0))
            step(dve.memset(v_s[:, :, 0:H * VW], 1.0))
            step(dve.memset(v_s[:, :, H * VW:], 0.0))
            dve.wait_ge(s_cact, 1)
            step(dve.tensor_scalar(c_tanh, c_tanh, 0.5, 0.5, ALU.mult, ALU.add))
            step(dve.tensor_tensor(c_silu, c_tanh, c_raw, ALU.mult))
            assert pre[0] == SILU_STEPS
            dve.wait_ge(s_const, 16 * CONST_DMAS)
            step(dve.tensor_copy(ident_b[:, :], ident[:, :]))
            dve.wait_ge(s_xln, 16)
            ln_stats(0, st1, mv1, ve1, s_ln1)
            ln_rows(0, xa, mv1, rstd1, s_ln1, s_rstd1)
            dve.wait_ge(s_wq, 16)
            step(dve.tensor_copy(wqkv_hi[:, :, :], wqkv_v))
            step(dve.tensor_tensor(wqkv_lo[:, :, :], wqkv_v, wqkv_hi[:, :, :].bitcast(F32), ALU.subtract))
            dve.wait_ge(s_modp, 1)
            mp = S[2][:, 0:6 * CT * NB].rearrange("p (k b) -> p b k", b=NB)
            tab = modB[:, :].rearrange("p (b k) -> p b k", k=MODS)
            for chunk, (dst, plus) in enumerate(((SA, 0.0), (CA, 1.0), (GA, 0.0), (SB, 0.0), (CB, 1.0), (GB, 0.0))):
                step(dve.tensor_scalar(tab[:, :, dst:dst + 2], mp[:, :, 2 * chunk:2 * chunk + 2], plus, None,
                                       ALU.add))
            for dst in (GA, GB):
                g = tab[:, :, dst:dst + 2]
                mag, sgn = (v.rearrange("p (b k) -> p b k", k=2) for v in (gate_mag, gate_sgn))
                step(dve.scalar_tensor_tensor(mag, g, -1.0, g, ALU.mult, ALU.max))
                step(dve.tensor_scalar(mag, mag, GATE_MIN, None, ALU.max))
                step(dve.tensor_scalar(sgn, g, 0.0, 2.0, ALU.is_ge, ALU.mult))
                step(dve.tensor_scalar(sgn, sgn, 1.0, None, ALU.subtract))
                step(dve.tensor_tensor(g, mag, sgn, ALU.mult))
            step(dve.tensor_tensor(tab[:, :, GPB:GPB + 2], tab[:, :, GA:GA + 2],
                                   pb_s[:, :].unsqueeze(1).broadcast_to([P, NB, 2]), ALU.mult))
            assert pre[0] == PRE_STEPS, pre[0]
            evacuate_h1(0, S[0:2])
            split_h1(0)
            rope(0, 0)
            rope(0, 1)
            v_bias(0)
            iteration(0, first=True)
            with dve.Fori(1, NB - 1) as b:
                iteration(b)
            iteration(NB - 1, last=True)
            for e in range(1, SLOTS):
                gated(NB - 1, e)
                times_up(NB - 1, e)
            add_y(NB - 1)


SILU_STEPS = 6
PRE_STEPS = SILU_STEPS + 3 + 6 + 10 + 1


def layouts(a):
    f32 = np.float32
    qkv = a["L0_attn_qkv_w"]
    wqk = qkv[:2 * C].reshape(2, H, HALF, 2, C).transpose(4, 0, 3, 2, 1).reshape(C, 2 * C)
    wqkv = np.concatenate([wqk, qkv[2 * C:].T], axis=1)
    qkb = a["L0_attn_qkv_b"][:2 * C].reshape(2, H, HALF, 2).transpose(2, 1, 0, 3).reshape(P, 4)
    pw = a["L0_attn_proj_w"].T.reshape(CT, 2, 4, HD, C).transpose(2, 1, 3, 0, 4)
    def cols(w):
        return w.reshape(C, 2, M).transpose(1, 0, 2)
    gate = np.concatenate([cols(a["L0_ffn_sw_gate"]), a["L0_ffn_w_gate"]])
    up = np.concatenate([cols(a["L0_ffn_sw_up"]), a["L0_ffn_w_up"]])
    gu = np.stack([gate, up], 1).reshape(SLOTS, 2, CT, P, M).transpose(0, 3, 1, 2, 4).reshape(SLOTS, P, 4 * M)
    down = np.concatenate([a["L0_ffn_sw_down"].reshape(2, M, C), a["L0_ffn_w_down"]])
    inv = f32(1.0) / f32(10000.0) ** (np.arange(0, HD, 2, dtype=f32) / f32(HD))
    freqs = np.arange(N, dtype=f32)[None, :] * np.repeat(inv, H)[:, None]
    tri = (np.arange(4)[None, :] < np.arange(4)[:, None]).astype(f32).reshape(16)
    return {
        "x": a["L0_attn_x"], "cT": a["L0_c"].T, "wmod": a["L0_wmod"], "wqkv": wqkv, "qkb": qkb,
        "vb": a["L0_attn_qkv_b"][2 * C:], "pw": pw.reshape(P, CT, C),
        "pb": a["L0_attn_proj_b"].reshape(CT, P).T, "gk": a["L0_ffn_gate_kernel"],
        "gb": a["L0_ffn_gate_bias"], "wffn": np.concatenate([gu, down], axis=2),
        "cosT": np.cos(freqs), "sinT": np.sin(freqs), "ident_in": np.eye(P, dtype=f32), "tri_in": tri,
    }


def kernel(**inputs):
    import concourse.bacc as bacc
    from concourse.bass_utils import run_bass_kernel_spmd

    nc = bacc.Bacc("TRN2", target_bir_lowering=False, num_devices=1)
    arrays = {k: np.ascontiguousarray(v) for k, v in layouts({k: np.asarray(v) for k, v in inputs.items()}).items()}
    args = {k: nc.dram_tensor(k, v.shape, F32, kind="ExternalInput").ap() for k, v in arrays.items()}
    out = nc.dram_tensor("out", (NB, N, C), F32, kind="ExternalOutput").ap()
    build(nc, **args, out=out)
    r = run_bass_kernel_spmd(nc, [arrays], core_ids=[0])
    return r.results[0]["out"]
```
